# Optimizing a Trainium2 kernel written in Bass

```python
import numpy as np
import jax
import jax.numpy as jnp

def _softmax(x, axis=-1):
    return jax.nn.softmax(x, axis=axis)

def _gelu(x):
    return jax.nn.gelu(x, approximate=True)

def _silu(x):
    return jax.nn.silu(x)

def _sigmoid(x):
    return jax.nn.sigmoid(x)

def _layernorm(x, axis=-1, eps=1e-05):
    m = jnp.mean(x, axis=axis, keepdims=True)
    v = jnp.var(x, axis=axis, keepdims=True)
    return (x - m) / jnp.sqrt(v + eps)

def _scatter_add(tgt, idx, src, axis=0):
    return tgt.at[idx].add(src)

def _segment_sum(src, seg, n):
    return jax.ops.segment_sum(src, seg, n)
kernel_name = 'mk_xattn_seq_d4_seqx_r4_b56f73'

def setup_inputs(seed: int=0):
    np.random.seed(seed)
    _w = jnp.asarray

    def _rec_inputs():
        import jax
        import jax.numpy as jnp
        _rk = jax.random.key(seed)
        x = -0.0002928 + 1 * jax.random.normal(jax.random.fold_in(_rk, 1), (4, 512, 512), jnp.float32)
        _lenS = 512 - jax.random.randint(jax.random.fold_in(_rk, 7), (4,), 0, max(1, 512 // 4) + 1, jnp.int32)
        _lenS2 = 1601 - jax.random.randint(jax.random.fold_in(_rk, 8), (4,), 0, max(1, 1601 // 4) + 1, jnp.int32)
        _ctx_2048P = jax.random.normal(jax.random.fold_in(_rk, 11), (4, 16, 512), jnp.float32)
        _ctx_2048c = jax.random.dirichlet(jax.random.fold_in(_rk, 511), 0.3 * jnp.ones((16,), jnp.float32), (4, 1601))
        _ctx_2048t = jnp.einsum('bsk,bkd->bsd', _ctx_2048c, _ctx_2048P)
        _ctx_2048t = _ctx_2048t * jax.lax.rsqrt(jnp.mean(jnp.square(_ctx_2048t)) + 1e-12) * 0.953939
        ctx_2048 = 0.000189249 + 0.0999589 * (_ctx_2048t + 0.3 * jax.random.normal(jax.random.fold_in(_rk, 611), (4, 1601, 512), jnp.float32))
        _validS = jnp.arange(512)[None, :] < _lenS[:, None]
        _validS2 = jnp.arange(1601)[None, :] < _lenS2[:, None]
        _causal = jnp.tril(jnp.ones((512, 512), dtype=bool))
        mask_BxS2_bf1 = jnp.ones((4, 1601), dtype=bool)
        mask_Bx1xSxS2_ff0 = jnp.where(jnp.ones((4, 1, 512, 1601), dtype=bool), 0.0, -1000000000.0).astype(jnp.float32)
        mask_BxS2_ik0 = jnp.where(jnp.broadcast_to(_validS2[:, :], (4, 1601)), 0, 1).astype(jnp.int32)
        return (x, ctx_2048, mask_BxS2_bf1, mask_Bx1xSxS2_ff0, mask_BxS2_ik0)
    x, ctx_2048, mask_BxS2_bf1, mask_Bx1xSxS2_ff0, mask_BxS2_ik0 = _rec_inputs()

    def _L0_xattn_setup():
        import jax, jax.numpy as jnp
        import numpy as np
        B, L, E, H = (4, 128, 512, 32)
        S = E // H
        EXTRA_MAA, EXTRA_DECAY = (32, 64)
        EPS = 1e-05

        def _ln(x, w, b):
            m = jnp.mean(x, axis=-1, keepdims=True)
            v = jnp.mean((x - m) ** 2, axis=-1, keepdims=True)
            return (x - m) * jax.lax.rsqrt(v + EPS) * w + b

        def _token_shift(xn, prev_row):
            first = (prev_row - xn[:, 0])[:, None]
            rest = xn[:, :-1] - xn[:, 1:]
            return jnp.concatenate([first, rest], axis=1)
        key = jax.random.key(seed)
        ks = jax.random.split(key, 24)
        rn = lambda k, shp, s=1.0: jax.random.normal(k, shp, dtype=jnp.float32) * s
        return dict(x=rn(ks[0], (B, L, E)), state=rn(ks[1], (B, 2 + S, E), 0.1), ln1_w=jnp.ones((E,), jnp.float32), ln1_b=jnp.zeros((E,), jnp.float32), ln2_w=jnp.ones((E,), jnp.float32), ln2_b=jnp.zeros((E,), jnp.float32), maa_x=rn(ks[2], (E,), 0.02), maa_w1=rn(ks[3], (E, 5 * EXTRA_MAA), 0.02), maa_w2=rn(ks[4], (5, EXTRA_MAA, E), 0.02), maa_stack=rn(ks[5], (5, E), 0.02), time_decay=rn(ks[6], (E,), 0.5), decay_w1=rn(ks[7], (E, EXTRA_DECAY), 0.02), decay_w2=rn(ks[8], (EXTRA_DECAY, E), 0.02), faaaa=rn(ks[9], (H, S), 0.1), Wr=rn(ks[10], (E, E), 0.02), Wk=rn(ks[11], (E, E), 0.02), Wv=rn(ks[12], (E, E), 0.02), Wg=rn(ks[13], (E, E), 0.02), Wo=rn(ks[14], (E, E), 0.02), gn_w=jnp.ones((E,), jnp.float32), gn_b=jnp.zeros((E,), jnp.float32), ffn_maa_k=rn(ks[15], (E,), 0.02), ffn_maa_r=rn(ks[16], (E,), 0.02), ffn_Wk=rn(ks[17], (E, E), 0.02), ffn_Wr=rn(ks[18], (E, E), 0.02), ffn_Wv=rn(ks[19], (E, E), 0.02), i=0)
    _L0_xattn_all = _L0_xattn_setup()
    _L0_xattn_in = {k: v for k, v in _L0_xattn_all.items() if k in ('ln1_w', 'ln1_b', 'ln2_w', 'ln2_b', 'maa_x', 'maa_w1', 'maa_w2', 'maa_stack', 'time_decay', 'decay_w1', 'decay_w2', 'faaaa', 'Wr', 'Wk', 'Wv', 'Wg', 'Wo', 'gn_w', 'gn_b', 'ffn_maa_k', 'ffn_maa_r', 'ffn_Wk', 'ffn_Wr', 'ffn_Wv')}
    del _L0_xattn_all

    def _L1_xattn_setup():
        import jax, jax.numpy as jnp
        import numpy as np
        HIDDEN = 512
        HEADS = 16
        HEAD_DIM = HIDDEN // HEADS
        LN_EPS = 1e-05
        GATE_INIT = 0.5

        def _layer_norm(x, gamma, beta):
            mu = jnp.mean(x, axis=-1, keepdims=True)
            var = jnp.mean(jnp.square(x - mu), axis=-1, keepdims=True)
            return (x - mu) * jax.lax.rsqrt(var + LN_EPS) * gamma + beta
        key = jax.random.key(seed)
        ks = jax.random.split(key, 8)
        B, T_TEXT, T_AUDIO = (4, 512, 375)
        s = 0.02
        return {'hidden_states': jax.random.normal(ks[0], (B, T_TEXT, HIDDEN), jnp.float32), 'audio_kv': jax.random.normal(ks[1], (B, T_AUDIO, HIDDEN), jnp.float32), 'audio_attention_mask': jnp.ones((B, T_AUDIO), dtype=bool), 'Wq': jax.random.normal(ks[2], (HIDDEN, HIDDEN), jnp.float32) * s, 'Wk': jax.random.normal(ks[3], (HIDDEN, HIDDEN), jnp.float32) * s, 'Wv': jax.random.normal(ks[4], (HIDDEN, HIDDEN), jnp.float32) * s, 'Wo': jax.random.normal(ks[5], (HIDDEN, HIDDEN), jnp.float32) * s, 'ln_gamma': jnp.ones((HIDDEN,), jnp.float32), 'ln_beta': jnp.zeros((HIDDEN,), jnp.float32), 'gate': jnp.array([GATE_INIT], jnp.float32)}
    _L1_xattn_all = _L1_xattn_setup()
    _L1_xattn_in = {k: v for k, v in _L1_xattn_all.items() if k in ('Wq', 'Wk', 'Wv', 'Wo', 'ln_gamma', 'ln_beta', 'gate')}
    del _L1_xattn_all

    def _L2_xattn_setup():
        import jax, jax.numpy as jnp
        import numpy as np
        H = 512
        NH = 32
        KVH = 8
        HD = H // NH
        GROUPS = NH // KVH
        EPS = 1e-06
        B, L, S = (4, 256, 256)

        def _gqa_forward(hidden_state, encoder_hidden_state, encoder_attention_mask, Wq, bq, Wk, bk, Wv, bv, Wo, bo, gamma, beta):
            b, l, _ = hidden_state.shape
            s = encoder_hidden_state.shape[1]
            q = hidden_state @ Wq + bq
            k = encoder_hidden_state @ Wk + bk
            v = encoder_hidden_state @ Wv + bv
            q = q.reshape(b, l, KVH, GROUPS, HD).transpose(0, 2, 3, 1, 4)
            k = k.reshape(b, s, KVH, HD).transpose(0, 2, 1, 3)
            v = v.reshape(b, s, KVH, HD).transpose(0, 2, 1, 3)
            scale = 1.0 / jnp.sqrt(jnp.asarray(HD, q.dtype))
            scores = jnp.einsum('bkgld,bksd->bkgls', q, k) * scale
            scores = scores + encoder_attention_mask[:, :, None, :, :]
            attn = jax.nn.softmax(scores, axis=-1)
            out = jnp.einsum('bkgls,bksd->bkgld', attn, v)
            out = out.transpose(0, 3, 1, 2, 4).reshape(b, l, H)
            out = out @ Wo + bo
            x = out + hidden_state
            mu = jnp.mean(x, axis=-1, keepdims=True)
            var = jnp.var(x, axis=-1, keepdims=True)
            return (x - mu) * jax.lax.rsqrt(var + EPS) * gamma + beta
        key = jax.random.key(seed)
        ks = jax.random.split(key, 12)
        sd = 0.02
        return {'hidden_state': jax.random.normal(ks[0], (B, L, H), jnp.float32), 'encoder_hidden_state': jax.random.normal(ks[1], (B, S, H), jnp.float32), 'encoder_attention_mask': jnp.zeros((B, 1, L, S), jnp.float32), 'Wq': jax.random.normal(ks[2], (H, H), jnp.float32) * sd, 'bq': jnp.zeros((H,), jnp.float32), 'Wk': jax.random.normal(ks[3], (H, KVH * HD), jnp.float32) * sd, 'bk': jnp.zeros((KVH * HD,), jnp.float32), 'Wv': jax.random.normal(ks[4], (H, KVH * HD), jnp.float32) * sd, 'bv': jnp.zeros((KVH * HD,), jnp.float32), 'Wo': jax.random.normal(ks[5], (H, H), jnp.float32) * sd, 'bo': jnp.zeros((H,), jnp.float32), 'gamma': jnp.ones((H,), jnp.float32), 'beta': jnp.zeros((H,), jnp.float32)}
    _L2_xattn_all = _L2_xattn_setup()
    _L2_xattn_in = {k: v for k, v in _L2_xattn_all.items() if k in ('Wq', 'bq', 'Wk', 'bk', 'Wv', 'bv', 'Wo', 'bo', 'gamma', 'beta')}
    del _L2_xattn_all

    def _L3_xattn_setup():
        import jax, jax.numpy as jnp
        import numpy as np
        B, P, K, H, NH = (4, 512, 64, 512, 16)
        DH = H // NH
        EPS = 1e-06

        def rmsnorm(x, w):
            var = jnp.mean(jnp.square(x), axis=-1, keepdims=True)
            return x * jax.lax.rsqrt(var + EPS) * w
        key = jax.random.key(seed)
        ks = jax.random.split(key, 12)
        s = 0.02
        return {'x': jax.random.normal(ks[0], (B, P, H), jnp.float32), 'latents': jax.random.normal(ks[1], (B, K, H), jnp.float32), 'attention_mask': jax.random.randint(ks[2], (B, P), 0, 2, jnp.int32), 'q_w': s * jax.random.normal(ks[3], (H, H), jnp.float32), 'q_b': jnp.zeros((H,), jnp.float32), 'kv_w': s * jax.random.normal(ks[4], (H, 2 * H), jnp.float32), 'kv_b': jnp.zeros((2 * H,), jnp.float32), 'out_w': s * jax.random.normal(ks[5], (H, H), jnp.float32), 'out_b': jnp.zeros((H,), jnp.float32), 'postnorm_w': jnp.ones((H,), jnp.float32), 'mlp_w1': s * jax.random.normal(ks[6], (H, 4 * H), jnp.float32), 'mlp_b1': jnp.zeros((4 * H,), jnp.float32), 'mlp_w2': s * jax.random.normal(ks[7], (4 * H, H), jnp.float32), 'mlp_b2': jnp.zeros((H,), jnp.float32)}
    _L3_xattn_all = _L3_xattn_setup()
    _L3_xattn_in = {k: v for k, v in _L3_xattn_all.items() if k in ('q_w', 'q_b', 'kv_w', 'kv_b', 'out_w', 'out_b', 'postnorm_w', 'mlp_w1', 'mlp_b1', 'mlp_w2', 'mlp_b2')}
    del _L3_xattn_all
    return {'x': x, 'ctx_2048': ctx_2048, 'mask_BxS2_bf1': mask_BxS2_bf1, 'mask_Bx1xSxS2_ff0': mask_Bx1xSxS2_ff0, 'mask_BxS2_ik0': mask_BxS2_ik0, 'L0_xattn_ln1_w': _L0_xattn_in['ln1_w'], 'L0_xattn_ln1_b': _L0_xattn_in['ln1_b'], 'L0_xattn_ln2_w': _L0_xattn_in['ln2_w'], 'L0_xattn_ln2_b': _L0_xattn_in['ln2_b'], 'L0_xattn_maa_x': _L0_xattn_in['maa_x'], 'L0_xattn_maa_w1': _L0_xattn_in['maa_w1'], 'L0_xattn_maa_w2': _L0_xattn_in['maa_w2'], 'L0_xattn_maa_stack': _L0_xattn_in['maa_stack'], 'L0_xattn_time_decay': _L0_xattn_in['time_decay'], 'L0_xattn_decay_w1': _L0_xattn_in['decay_w1'], 'L0_xattn_decay_w2': _L0_xattn_in['decay_w2'], 'L0_xattn_faaaa': _L0_xattn_in['faaaa'], 'L0_xattn_Wr': _L0_xattn_in['Wr'], 'L0_xattn_Wk': _L0_xattn_in['Wk'], 'L0_xattn_Wv': _L0_xattn_in['Wv'], 'L0_xattn_Wg': _L0_xattn_in['Wg'], 'L0_xattn_Wo': _L0_xattn_in['Wo'], 'L0_xattn_gn_w': _L0_xattn_in['gn_w'], 'L0_xattn_gn_b': _L0_xattn_in['gn_b'], 'L0_xattn_ffn_maa_k': _L0_xattn_in['ffn_maa_k'], 'L0_xattn_ffn_maa_r': _L0_xattn_in['ffn_maa_r'], 'L0_xattn_ffn_Wk': _L0_xattn_in['ffn_Wk'], 'L0_xattn_ffn_Wr': _L0_xattn_in['ffn_Wr'], 'L0_xattn_ffn_Wv': _L0_xattn_in['ffn_Wv'], 'L1_xattn_Wq': _L1_xattn_in['Wq'], 'L1_xattn_Wk': _L1_xattn_in['Wk'], 'L1_xattn_Wv': _L1_xattn_in['Wv'], 'L1_xattn_Wo': _L1_xattn_in['Wo'], 'L1_xattn_ln_gamma': _L1_xattn_in['ln_gamma'], 'L1_xattn_ln_beta': _L1_xattn_in['ln_beta'], 'L1_xattn_gate': _L1_xattn_in['gate'], 'L2_xattn_Wq': _L2_xattn_in['Wq'], 'L2_xattn_bq': _L2_xattn_in['bq'], 'L2_xattn_Wk': _L2_xattn_in['Wk'], 'L2_xattn_bk': _L2_xattn_in['bk'], 'L2_xattn_Wv': _L2_xattn_in['Wv'], 'L2_xattn_bv': _L2_xattn_in['bv'], 'L2_xattn_Wo': _L2_xattn_in['Wo'], 'L2_xattn_bo': _L2_xattn_in['bo'], 'L2_xattn_gamma': _L2_xattn_in['gamma'], 'L2_xattn_beta': _L2_xattn_in['beta'], 'L3_xattn_q_w': _L3_xattn_in['q_w'], 'L3_xattn_q_b': _L3_xattn_in['q_b'], 'L3_xattn_kv_w': _L3_xattn_in['kv_w'], 'L3_xattn_kv_b': _L3_xattn_in['kv_b'], 'L3_xattn_out_w': _L3_xattn_in['out_w'], 'L3_xattn_out_b': _L3_xattn_in['out_b'], 'L3_xattn_postnorm_w': _L3_xattn_in['postnorm_w'], 'L3_xattn_mlp_w1': _L3_xattn_in['mlp_w1'], 'L3_xattn_mlp_b1': _L3_xattn_in['mlp_b1'], 'L3_xattn_mlp_w2': _L3_xattn_in['mlp_w2'], 'L3_xattn_mlp_b2': _L3_xattn_in['mlp_b2']}

def reference(x, ctx_2048, mask_BxS2_bf1, mask_Bx1xSxS2_ff0, mask_BxS2_ik0, L0_xattn_ln1_w, L0_xattn_ln1_b, L0_xattn_ln2_w, L0_xattn_ln2_b, L0_xattn_maa_x, L0_xattn_maa_w1, L0_xattn_maa_w2, L0_xattn_maa_stack, L0_xattn_time_decay, L0_xattn_decay_w1, L0_xattn_decay_w2, L0_xattn_faaaa, L0_xattn_Wr, L0_xattn_Wk, L0_xattn_Wv, L0_xattn_Wg, L0_xattn_Wo, L0_xattn_gn_w, L0_xattn_gn_b, L0_xattn_ffn_maa_k, L0_xattn_ffn_maa_r, L0_xattn_ffn_Wk, L0_xattn_ffn_Wr, L0_xattn_ffn_Wv, L1_xattn_Wq, L1_xattn_Wk, L1_xattn_Wv, L1_xattn_Wo, L1_xattn_ln_gamma, L1_xattn_ln_beta, L1_xattn_gate, L2_xattn_Wq, L2_xattn_bq, L2_xattn_Wk, L2_xattn_bk, L2_xattn_Wv, L2_xattn_bv, L2_xattn_Wo, L2_xattn_bo, L2_xattn_gamma, L2_xattn_beta, L3_xattn_q_w, L3_xattn_q_b, L3_xattn_kv_w, L3_xattn_kv_b, L3_xattn_out_w, L3_xattn_out_b, L3_xattn_postnorm_w, L3_xattn_mlp_w1, L3_xattn_mlp_b1, L3_xattn_mlp_w2, L3_xattn_mlp_b2):
    import jax
    import jax.numpy as jnp

    def _L0_xattn_ref(x, state, ln1_w, ln1_b, ln2_w, ln2_b, maa_x, maa_w1, maa_w2, maa_stack, time_decay, decay_w1, decay_w2, faaaa, Wr, Wk, Wv, Wg, Wo, gn_w, gn_b, ffn_maa_k, ffn_maa_r, ffn_Wk, ffn_Wr, ffn_Wv, i):
        import jax, jax.numpy as jnp
        import numpy as np
        B, L, E, H = (4, 128, 512, 32)
        S = E // H
        EXTRA_MAA, EXTRA_DECAY = (32, 64)
        EPS = 1e-05

        def _ln(x, w, b):
            m = jnp.mean(x, axis=-1, keepdims=True)
            v = jnp.mean((x - m) ** 2, axis=-1, keepdims=True)
            return (x - m) * jax.lax.rsqrt(v + EPS) * w + b

        def _token_shift(xn, prev_row):
            first = (prev_row - xn[:, 0])[:, None]
            rest = xn[:, :-1] - xn[:, 1:]
            return jnp.concatenate([first, rest], axis=1)
        b, l = (x.shape[0], x.shape[1])
        i0 = (2 + S) * i + 0
        i1 = (2 + S) * i + 1
        xn = _ln(x, ln1_w, ln1_b)
        sx = _token_shift(xn, state[:, i1])
        xxx = jnp.tanh((xn + sx * maa_x) @ maa_w1).reshape(b, l, 5, 1, EXTRA_MAA)
        xxx = jnp.matmul(xxx, maa_w2).reshape(b, l, 5, E)
        x5 = xn[:, :, None] + sx[:, :, None] * (maa_stack + xxx)
        w = jnp.exp(-jnp.exp(time_decay + jnp.tanh(x5[:, :, 1] @ decay_w1) @ decay_w2))
        w = w.reshape(b, l, H, S)
        r = (x5[:, :, 3] @ Wr.T).reshape(b, l, H, S)
        k = (x5[:, :, 0] @ Wk.T).reshape(b, l, H, S)
        v = (x5[:, :, 2] @ Wv.T).reshape(b, l, H, S)
        g = jax.nn.silu(x5[:, :, 4] @ Wg.T)
        s0 = state[:, (2 + S) * i + 2:(2 + S) * (i + 1)].reshape(b, H, S, S)
        u = faaaa[None, :, :, None]

        def step(s, rkvw):
            r_t, k_t, v_t, w_t = rkvw
            a = k_t[:, :, :, None] * v_t[:, :, None, :]
            out = jnp.einsum('bhk,bhkd->bhd', r_t, u * a + s)
            return (a + w_t[:, :, :, None] * s, out)
        xs = tuple((jnp.moveaxis(t, 1, 0) for t in (r, k, v, w)))
        _, outs = jax.lax.scan(step, s0, xs)
        att = jnp.moveaxis(outs, 0, 1).reshape(b, l, E)
        a4 = att.reshape(b, l, H, S)
        m = jnp.mean(a4, axis=-1, keepdims=True)
        var = jnp.mean((a4 - m) ** 2, axis=-1, keepdims=True)
        att = ((a4 - m) * jax.lax.rsqrt(var + EPS)).reshape(b, l, E) * gn_w + gn_b
        x = x + att * g @ Wo.T
        xn2 = _ln(x, ln2_w, ln2_b)
        sx2 = _token_shift(xn2, state[:, i0])
        xk = xn2 + sx2 * ffn_maa_k
        xr = xn2 + sx2 * ffn_maa_r
        rr = jax.nn.sigmoid(xr @ ffn_Wr.T)
        kk = jnp.square(jax.nn.relu(xk @ ffn_Wk.T))
        x = x + rr * (kk @ ffn_Wv.T)
        return x

    def _L1_xattn_ref(hidden_states, audio_kv, audio_attention_mask, Wq, Wk, Wv, Wo, ln_gamma, ln_beta, gate):
        import jax, jax.numpy as jnp
        import numpy as np
        HIDDEN = 512
        HEADS = 16
        HEAD_DIM = HIDDEN // HEADS
        LN_EPS = 1e-05
        GATE_INIT = 0.5

        def _layer_norm(x, gamma, beta):
            mu = jnp.mean(x, axis=-1, keepdims=True)
            var = jnp.mean(jnp.square(x - mu), axis=-1, keepdims=True)
            return (x - mu) * jax.lax.rsqrt(var + LN_EPS) * gamma + beta
        B, Tt, D = hidden_states.shape
        Ta = audio_kv.shape[1]
        scale = HEAD_DIM ** (-0.5)
        a = _layer_norm(audio_kv, ln_gamma, ln_beta)
        Q = (hidden_states @ Wq.T).reshape(B, Tt, HEADS, HEAD_DIM).transpose(0, 2, 1, 3)
        K = (a @ Wk.T).reshape(B, Ta, HEADS, HEAD_DIM).transpose(0, 2, 1, 3)
        V = (a @ Wv.T).reshape(B, Ta, HEADS, HEAD_DIM).transpose(0, 2, 1, 3)
        scores = jnp.einsum('bhtd,bhsd->bhts', Q, K) * scale
        mask = audio_attention_mask[:, None, None, :]
        scores = jnp.where(mask, scores, jnp.float32(-jnp.inf))
        attn = jax.nn.softmax(scores, axis=-1)
        out = jnp.einsum('bhts,bhsd->bhtd', attn, V)
        out = out.transpose(0, 2, 1, 3).reshape(B, Tt, D)
        out = out @ Wo.T
        return hidden_states + jnp.tanh(gate) * out

    def _L2_xattn_ref(hidden_state, encoder_hidden_state, encoder_attention_mask, Wq, bq, Wk, bk, Wv, bv, Wo, bo, gamma, beta):
        import jax, jax.numpy as jnp
        import numpy as np
        H = 512
        NH = 32
        KVH = 8
        HD = H // NH
        GROUPS = NH // KVH
        EPS = 1e-06
        B, L, S = (4, 256, 256)

        def _gqa_forward(hidden_state, encoder_hidden_state, encoder_attention_mask, Wq, bq, Wk, bk, Wv, bv, Wo, bo, gamma, beta):
            b, l, _ = hidden_state.shape
            s = encoder_hidden_state.shape[1]
            q = hidden_state @ Wq + bq
            k = encoder_hidden_state @ Wk + bk
            v = encoder_hidden_state @ Wv + bv
            q = q.reshape(b, l, KVH, GROUPS, HD).transpose(0, 2, 3, 1, 4)
            k = k.reshape(b, s, KVH, HD).transpose(0, 2, 1, 3)
            v = v.reshape(b, s, KVH, HD).transpose(0, 2, 1, 3)
            scale = 1.0 / jnp.sqrt(jnp.asarray(HD, q.dtype))
            scores = jnp.einsum('bkgld,bksd->bkgls', q, k) * scale
            scores = scores + encoder_attention_mask[:, :, None, :, :]
            attn = jax.nn.softmax(scores, axis=-1)
            out = jnp.einsum('bkgls,bksd->bkgld', attn, v)
            out = out.transpose(0, 3, 1, 2, 4).reshape(b, l, H)
            out = out @ Wo + bo
            x = out + hidden_state
            mu = jnp.mean(x, axis=-1, keepdims=True)
            var = jnp.var(x, axis=-1, keepdims=True)
            return (x - mu) * jax.lax.rsqrt(var + EPS) * gamma + beta
        return _gqa_forward(hidden_state, encoder_hidden_state, encoder_attention_mask, Wq, bq, Wk, bk, Wv, bv, Wo, bo, gamma, beta)

    def _L3_xattn_ref(x, latents, attention_mask, q_w, q_b, kv_w, kv_b, out_w, out_b, postnorm_w, mlp_w1, mlp_b1, mlp_w2, mlp_b2):
        import jax, jax.numpy as jnp
        import numpy as np
        B, P, K, H, NH = (4, 512, 64, 512, 16)
        DH = H // NH
        EPS = 1e-06

        def rmsnorm(x, w):
            var = jnp.mean(jnp.square(x), axis=-1, keepdims=True)
            return x * jax.lax.rsqrt(var + EPS) * w
        b, p, _ = x.shape
        k_len = latents.shape[1]
        residual = latents
        h = jnp.concatenate([x, latents], axis=1)
        q = (latents @ q_w + q_b).reshape(b, k_len, NH, DH)
        kv = (h @ kv_w + kv_b).reshape(b, p + k_len, NH, DH, 2)
        kmat, v = (kv[..., 0], kv[..., 1])
        attn = jnp.einsum('bkhd,bnhd->bhkn', q, kmat) / DH
        full_mask = jnp.concatenate([attention_mask.astype(bool), jnp.ones((b, k_len), bool)], axis=-1)
        attn = jnp.where(full_mask[:, None, None, :], attn, -jnp.inf)
        attn = jax.nn.softmax(attn.astype(jnp.float32), axis=-1).astype(q.dtype)
        attn_out = jnp.einsum('bhkn,bnhd->bkhd', attn, v).reshape(b, k_len, H)
        attn_out = attn_out @ out_w + out_b + residual
        out = rmsnorm(attn_out, postnorm_w)
        out = jax.nn.gelu(out @ mlp_w1 + mlp_b1) @ mlp_w2 + mlp_b2
        return out + residual
    x = _L0_xattn_ref(x, ctx_2048, L0_xattn_ln1_w, L0_xattn_ln1_b, L0_xattn_ln2_w, L0_xattn_ln2_b, L0_xattn_maa_x, L0_xattn_maa_w1, L0_xattn_maa_w2, L0_xattn_maa_stack, L0_xattn_time_decay, L0_xattn_decay_w1, L0_xattn_decay_w2, L0_xattn_faaaa, L0_xattn_Wr, L0_xattn_Wk, L0_xattn_Wv, L0_xattn_Wg, L0_xattn_Wo, L0_xattn_gn_w, L0_xattn_gn_b, L0_xattn_ffn_maa_k, L0_xattn_ffn_maa_r, L0_xattn_ffn_Wk, L0_xattn_ffn_Wr, L0_xattn_ffn_Wv, 0)
    x = _L1_xattn_ref(x, ctx_2048, mask_BxS2_bf1, L1_xattn_Wq, L1_xattn_Wk, L1_xattn_Wv, L1_xattn_Wo, L1_xattn_ln_gamma, L1_xattn_ln_beta, L1_xattn_gate)
    x = _L2_xattn_ref(x, ctx_2048, mask_Bx1xSxS2_ff0, L2_xattn_Wq, L2_xattn_bq, L2_xattn_Wk, L2_xattn_bk, L2_xattn_Wv, L2_xattn_bv, L2_xattn_Wo, L2_xattn_bo, L2_xattn_gamma, L2_xattn_beta)
    x = _L3_xattn_ref(ctx_2048, x, mask_BxS2_ik0, L3_xattn_q_w, L3_xattn_q_b, L3_xattn_kv_w, L3_xattn_kv_b, L3_xattn_out_w, L3_xattn_out_b, L3_xattn_postnorm_w, L3_xattn_mlp_w1, L3_xattn_mlp_b1, L3_xattn_mlp_w2, L3_xattn_mlp_b2)
    return x

_drawn_inputs = setup_inputs


def setup_inputs(seed=0):
    import zlib

    import numpy as np

    out = dict(_drawn_inputs(seed))
    spreads = {'L0_xattn_ln1_w': (1.0, 0.2),
     'L0_xattn_ln1_b': (0.0, 0.268),
     'L0_xattn_ln2_w': (1.0, 0.6),
     'L0_xattn_ln2_b': (0.0, 0.8),
     'L0_xattn_gn_w': (1.0, 0.6),
     'L0_xattn_gn_b': (0.0, 0.685),
     'L1_xattn_ln_gamma': (1.0, 0.6),
     'L1_xattn_ln_beta': (0.0, 0.8),
     'L2_xattn_bq': (0.0, 2.0),
     'L2_xattn_bk': (0.0, 2.0),
     'L2_xattn_bv': (0.0, 0.1),
     'L2_xattn_bo': (0.0, 0.1),
     'L2_xattn_gamma': (1.0, 0.2),
     'L2_xattn_beta': (0.0, 0.1),
     'L3_xattn_q_b': (0.0, 0.8),
     'L3_xattn_kv_b': (0.0, 0.8),
     'L3_xattn_out_b': (0.0, 1.423),
     'L3_xattn_postnorm_w': (1.0, 0.2),
     'L3_xattn_mlp_b1': (0.0, 0.1),
     'L3_xattn_mlp_b2': (0.0, 0.1)}
    factors = {'L0_xattn_maa_x': 8.0,
     'L0_xattn_maa_w1': 2.917,
     'L0_xattn_maa_w2': 2.942,
     'L0_xattn_maa_stack': 6.423,
     'L0_xattn_decay_w1': 8.0,
     'L0_xattn_decay_w2': 8.0,
     'L0_xattn_faaaa': 3.03,
     'L0_xattn_ffn_maa_k': 8.0,
     'L0_xattn_ffn_maa_r': 8.0,
     'L0_xattn_ffn_Wr': 4.201,
     'L1_xattn_Wq': 8.0,
     'L1_xattn_Wk': 8.0,
     'L2_xattn_Wq': 8.0,
     'L2_xattn_Wk': 8.0,
     'L2_xattn_Wv': 5.64,
     'L3_xattn_q_w': 8.0,
     'L3_xattn_kv_w': 8.0,
     'L3_xattn_out_w': 5.034}
    for name, (base, spread) in spreads.items():
        noise = np.random.default_rng([zlib.crc32(name.encode()), seed]).standard_normal(out[name].shape)
        drawn = base * np.exp(spread * noise) if base else spread * noise
        out[name] = jnp.asarray(drawn.astype(out[name].dtype))
    for name, factor in factors.items():
        out[name] = (out[name] * factor).astype(out[name].dtype)
    return out
```

```python
from contextlib import ExitStack

import concourse.bass as bass
from concourse import mybir

F32, F16 = mybir.dt.float32, mybir.dt.float16
U8, I32 = mybir.dt.uint8, mybir.dt.int32
ALU, ACT, AX = mybir.AluOpType, mybir.ActivationFunctionType, mybir.AxisListType

P = 128
B, T, E = 4, 512, 512
C = E // P
S2 = 1601
KT = 512
FULL, TAIL = S2 // KT, S2 % KT
HS = 16
MASKED = 32768.0
QUAD = 4


class Phase:

    def __init__(self, nc, ctx, tag):
        self.nc, self.ctx, self.tag, self.sems = nc, ctx, tag, []

    def sb(self, name, shape, dt=F32):
        return self.ctx.enter_context(self.nc.sbuf_tensor(f"{self.tag}_{name}", shape, dt))

    def ps(self, name, shape, dt=F32):
        return self.ctx.enter_context(self.nc.psum_tensor(f"{self.tag}_{name}", shape, dt))

    def sem(self, name):
        s = self.ctx.enter_context(self.nc.semaphore(f"{self.tag}_{name}"))
        self.sems.append(s)
        return s

    def renew(self):
        self.nc.all_engine_barrier()
        for s in self.sems:
            self.nc.sync.sem_clear(s)
        self.nc.all_engine_barrier()


class Chain:

    def __init__(self, eng, sem):
        self.eng, self.sem, self.n = eng, sem, 0

    def __call__(self, ins):
        ins.then_inc(self.sem, 1)
        self.n += 1
        self.eng.wait_ge(self.sem, self.n)


class Banks:

    def __init__(self, nc, pe, psum, product, drained):
        self.nc, self.pe, self.psum, self.product, self.drained, self.j = nc, pe, psum, product, drained, 0

    def __call__(self, pairs, m=P, n=T):
        if self.j >= 8:
            self.pe.wait_ge(self.drained, self.j - 7)
        out = self.psum[0:m, self.j % 8, 0:n]
        last = len(pairs) - 1
        for i, (lhsT, rhs) in enumerate(pairs):
            ins = self.nc.tensor.matmul(out, lhsT, rhs, start=i == 0, stop=i == last)
        ins.then_inc(self.product, 1)
        self.j += 1


class Drains:

    def __init__(self, nc, act, psum, product, drained):
        self.nc, self.act, self.psum, self.product, self.drained, self.j = nc, act, psum, product, drained, 0

    def __call__(self, out, func, m=P, n=T, **kw):
        self.act.wait_ge(self.product, self.j + 1)
        self.nc.scalar.activation(out, self.psum[0:m, self.j % 8, 0:n], func, **kw).then_inc(self.drained, 1)
        self.j += 1


def bc(ap, n):
    return ap.unsqueeze(1).broadcast_to([ap.shape[0], n, ap.shape[1]])


def load_weights(sp, sem, pairs):
    for dst, src in pairs:
        sp.dma_start(dst, src).then_inc(sem, 16)
    sp.wait_ge(sem, 16 * len(pairs))


def chunked(w):
    return w.rearrange("(c p) n -> p c n", p=P)


def column(v):
    return v


def setup(nc, ctx, w):
    ph = Phase(nc, ctx, "const")
    k = {}
    k["mean"] = ph.sb("mean", [P, P])
    k["ones"] = ph.sb("ones", [P, P])
    k["eps5"] = ph.sb("eps5", [P, 1])
    k["eps6"] = ph.sb("eps6", [P, 1])
    k["ident"] = ph.sb("ident", [P, P])
    k["sel"] = ph.sb("sel", [P, HS, P])
    k["red"] = ph.sb("red", [P, HS, P])
    k["head"] = ph.sb("head", [P, P])
    k["headmean"] = ph.sb("headmean", [P, P])
    loaded, made, step, stored = ph.sem("loaded"), ph.sem("made"), ph.sem("step"), ph.sem("stored")
    with ExitStack() as short:
        rows = Phase(nc, short, "masks")
        m8 = rows.sb("m8", [B, S2], U8)
        m32 = rows.sb("m32", [B, S2], I32)
        keep = rows.sb("keep", [B, S2])
        row1 = rows.sb("row1", [B, S2], F16)
        row3 = rows.sb("row3", [B, S2], F16)
        block = short.enter_context(nc.Block())

        @block.sync
        def _(sp):
            sp.dma_start(m8[:], w["mask1"]).then_inc(loaded, 16)
            sp.dma_start(m32[:], w["mask3"]).then_inc(loaded, 16)
            sp.dma_start(k["ident"][:], w["c_ident"]).then_inc(loaded, 16)
            sp.dma_start(k["sel"][:], w["c_sel"]).then_inc(loaded, 16)
            sp.dma_start(k["red"][:], w["c_red"]).then_inc(loaded, 16)
            sp.dma_start(k["head"][:], w["c_head"]).then_inc(loaded, 16)
            sp.wait_ge(made, 1)
            for name, row in (("km1", row1), ("km3", row3)):
                for g in range(w[name].shape[1]):
                    sp.dma_start(w[name][:, g, :], row[:]).then_inc(stored, 16)
            sp.wait_ge(stored, 16 * 2 * QUAD)

        @block.vector
        def _(dve):
            link = Chain(dve, step)
            link(nc.vector.memset(k["mean"][:], 1.0 / E))
            link(nc.vector.memset(k["ones"][:], 1.0))
            link(nc.vector.memset(k["eps5"][:], 1e-5))
            link(nc.vector.memset(k["eps6"][:], 1e-6))
            dve.wait_ge(loaded, 16 * 6)
            link(nc.vector.tensor_scalar(k["headmean"][:], k["head"][:], 1.0 / HS, None, ALU.mult))
            for m, row in ((m8, row1), (m32, row3)):
                link(nc.vector.tensor_copy(keep[:], m[:]))
                link(nc.vector.tensor_scalar(keep[:], keep[:], 0.0, MASKED, ALU.not_equal, ALU.mult))
                link(nc.vector.tensor_scalar(row[:], keep[:], MASKED, None, ALU.subtract))
            nc.vector.memset(m8[:], 0).then_inc(made, 1)
    ph.renew()
    return k


def rwkv_inputs(nc, w, k):
    with ExitStack() as ctx:
        ph = Phase(nc, ctx, "mix")
        W = {n: ph.sb(n, [P, C, E]) for n in ("Wr", "Wk", "Wv", "Wg")}
        w1 = ph.sb("w1", [P, C, 160])
        w2 = ph.sb("w2", [P, E])
        w2g = ph.sb("w2g", [32, E])
        dw1 = ph.sb("dw1", [P, C, 64])
        dw2 = ph.sb("dw2", [64, E])
        lnw, lnb, mx, td = (ph.sb(n, [P, C]) for n in ("lnw", "lnb", "mx", "td"))
        stack = ph.sb("stack", [P, 5, C])
        x, xc, sq = ph.sb("x", [P, C, T]), ph.sb("xc", [P, C, T]), ph.sb("sq", [P, C, T])
        xn = ph.sb("xn", [P, C, T + 1])
        prev = ph.sb("prev", [P, C])
        dx, u = ph.sb("dx", [P, C, T]), ph.sb("u", [P, C, T])
        mean, rstd = ph.sb("mean", [P, T]), ph.sb("rstd", [P, T])
        th, thg, dh_ = ph.sb("th", [P, T]), ph.sb("thg", [32, T]), ph.sb("dh", [64, T])
        mixed = [ph.sb(f"mixed{i}", [P, C, T]) for i in range(2)]
        y = [ph.sb(f"y{i}", [P, C, T]) for i in range(2)]
        psum = ph.ps("psum", [P, 8, T])
        loaded, product, drained, step = ph.sem("loaded"), ph.sem("product"), ph.sem("drained"), ph.sem("step")
        normed, squared, shifted, mixedup, ready = (ph.sem(n) for n in ("normed", "squared", "shifted", "mixedup", "ready"))
        centred, decays = ph.sem("centred"), ph.sem("decays")
        stored = [ph.sem(f"stored{i}") for i in range(2)]
        ORDER = (1, 0, 2, 3, 4)
        DEST = {0: "s_k", 1: "s_w", 2: "s_v", 3: "s_r", 4: "s_g"}
        WEIGHT = {0: "Wk", 2: "Wv", 3: "Wr", 4: "Wg"}

        with nc.Block() as block:
            @block.sync
            def _(sp):
                load_weights(sp, loaded, [(W[n][:], chunked(w[n + "0"])) for n in W] + [
                    (w1[:], chunked(w["maa_w1"])), (w2[:], w["maa_w2"][0:P, :]), (w2g[:], w["maa_w2"][P:P + 32, :]),
                    (dw1[:], chunked(w["decay_w1"])), (dw2[:], w["decay_w2"]), (lnw[:], column(w["ln1_w"])),
                    (lnb[:], column(w["ln1_b"])), (mx[:], column(w["maa_x"])), (td[:], column(w["time_decay"])),
                    (stack[:], w["maa_stack"])])
        ph.renew()

        first, at = {}, 4
        for n, i in enumerate(ORDER):
            if n == 0:
                first["mix", i] = at
                at += C
            if n + 1 < 5:
                first["mix", ORDER[n + 1]] = at
                at += C
            first["own", i] = at
            at += 1 + C if i == 1 else C

        with nc.Fori(0, B) as b:
            with nc.Block() as block:
                @block.sync
                def _(sp):
                    sp.dma_start(x[:], w["x_t"][b].rearrange("(c p) t -> p c t", p=P)).then_inc(loaded, 16)
                    sp.dma_start(prev[:], w["prev1"][b]).then_inc(loaded, 16)
                    for n, i in enumerate(ORDER):
                        sp.wait_ge(drained, first["own", i] + (1 + C if i == 1 else C))
                        if i == 1:
                            sp.wait_ge(decays, 1)
                        sp.dma_start(w[DEST[i]][b].rearrange("c p t -> p c t"), y[n % 2][:]).then_inc(stored[n % 2], 16)
                    sp.wait_ge(stored[0], 16 * 3)
                    sp.wait_ge(stored[1], 16 * 2)

                @block.tensor
                def _(pe):
                    group = Banks(nc, pe, psum, product, drained)
                    pe.wait_ge(loaded, 32)
                    group([(k["mean"][:], x[:, c, :]) for c in range(C)])
                    pe.wait_ge(squared, 1)
                    group([(k["mean"][:], sq[:, c, :]) for c in range(C)])
                    pe.wait_ge(shifted, 1)
                    group([(w1[:, c, 0:P], u[:, c, :]) for c in range(C)])
                    group([(w1[:, c, P:160], u[:, c, :]) for c in range(C)], m=32)

                    def mix(i):
                        for c in range(C):
                            f = slice(c * P, (c + 1) * P)
                            if i < 4:
                                r = slice(32 * i, 32 * i + 32)
                                group([(w2[r, f], th[r, :])])
                            else:
                                group([(w2g[:, f], thg[:])])

                    pe.wait_ge(drained, 4)
                    mix(ORDER[0])
                    for n, i in enumerate(ORDER):
                        if n + 1 < 5:
                            mix(ORDER[n + 1])
                        pe.wait_ge(mixedup, n + 1)
                        src = mixed[n % 2]
                        if i == 1:
                            group([(dw1[:, c, :], src[:, c, :]) for c in range(C)], m=64)
                            pe.wait_ge(drained, group.j)
                            for o in range(C):
                                group([(dw2[:, o * P:(o + 1) * P], dh_[:])])
                        else:
                            for o in range(C):
                                group([(W[WEIGHT[i]][:, c, o * P:(o + 1) * P], src[:, c, :]) for c in range(C)])

                @block.scalar
                def _(act):
                    drain = Drains(nc, act, psum, product, drained)
                    drain(mean[:], ACT.Identity)
                    act.wait_ge(centred, 1)
                    nc.scalar.activation(sq[:], xc[:], ACT.Square).then_inc(squared, 1)
                    drain(rstd[:], ACT.Sqrt, bias=k["eps5"][:])
                    drain(th[:], ACT.Tanh)
                    drain(thg[:], ACT.Tanh, m=32)

                    def mix(n, i):
                        dst = (sq, u)[n % 2]
                        if n >= 2:
                            act.wait_ge(mixedup, n - 1)
                        for c in range(C):
                            drain(dst[:, c, :], ACT.Identity, bias=stack[:, i, c:c + 1])

                    mix(0, ORDER[0])
                    for n, i in enumerate(ORDER):
                        if n + 1 < 5:
                            mix(n + 1, ORDER[n + 1])
                        if n >= 2:
                            act.wait_ge(stored[n % 2], 16 * (n // 2))
                        dst = y[n % 2]
                        if i == 1:
                            drain(dh_[:], ACT.Tanh, m=64)
                            for o in range(C):
                                drain(dst[:, o, :], ACT.Exp, bias=td[:, o:o + 1])
                            act.wait_ge(drained, drain.j)
                            nc.scalar.activation(dst[:], dst[:], ACT.Exp, scale=-1.0).then_inc(decays, 1)
                        else:
                            for o in range(C):
                                drain(dst[:, o, :], ACT.Silu if i == 4 else ACT.Identity)

                @block.vector
                def _(dve):
                    link = Chain(dve, step)
                    dve.wait_ge(loaded, 32)
                    link(nc.vector.tensor_copy(xn[:, :, 0], prev[:]))
                    dve.wait_ge(drained, 1)
                    nc.vector.tensor_tensor(xc[:], x[:], bc(mean[:], C), ALU.subtract).then_inc(centred, 1)
                    dve.wait_ge(centred, 1)
                    dve.wait_ge(drained, 2)
                    link(nc.vector.reciprocal(rstd[:], rstd[:]))
                    link(nc.vector.tensor_tensor(xc[:], xc[:], bc(rstd[:], C), ALU.mult))
                    for c in range(C):
                        link(nc.vector.tensor_scalar(xn[:, c, 1:], xc[:, c, :], lnw[:, c:c + 1], lnb[:, c:c + 1],
                                                     ALU.mult, ALU.add))
                    link(nc.vector.tensor_tensor(dx[:], xn[:, :, 0:T], xn[:, :, 1:], ALU.subtract))
                    for c in range(C):
                        ins = nc.vector.scalar_tensor_tensor(u[:, c, :], dx[:, c, :], mx[:, c:c + 1], xn[:, c, 1:],
                                                             ALU.mult, ALU.add)
                        link(ins) if c < C - 1 else ins.then_inc(shifted, 1)
                    for n, i in enumerate(ORDER):
                        dve.wait_ge(drained, first["mix", i] + C)
                        if n >= 2:
                            j = ORDER[n - 2]
                            dve.wait_ge(product, first["own", j] + (1 if j == 1 else C))
                        src, dst = (sq, u)[n % 2], mixed[n % 2]
                        link(nc.vector.tensor_tensor(dst[:], src[:], dx[:], ALU.mult))
                        nc.vector.tensor_tensor(dst[:], dst[:], xn[:, :, 1:], ALU.add).then_inc(mixedup, 1)
            ph.renew()


def recurrence(nc, w, k):
    with ExitStack() as ctx:
        ph = Phase(nc, ctx, "scan")
        src = {n: [ph.sb(f"{n}{i}", [P, T]) for i in range(2)] for n in "rkvw"}
        s0 = ph.sb("initial", [P, C, HS])
        bonus = ph.sb("bonus", [P, C])
        A = [ph.sb(f"a{i}", [P, T]) for i in range(2)]
        S = [ph.sb(f"states{i}", [P, T + 1]) for i in range(3)]
        Z = [ph.sb(f"z{i}", [P, T]) for i in range(3)]
        ruk = ph.sb("ruk", [P, T])
        bv = ph.sb("bv", [P, T])
        o = [ph.sb(f"o{i}", [P, T]) for i in range(2)]
        vb = ph.ps("vb", [P, 4, T])
        acc = ph.ps("acc", [P, 2, T])
        pb = ph.ps("pb", [P, T])
        loaded = [ph.sem(f"loaded{i}") for i in range(2)]
        first, spread, mul, scanned, zdone, reduced, rukdone, bonused, outdone, step, seeded = (
            ph.sem(n) for n in ("first", "spread", "mul", "scanned", "zdone", "reduced", "rukdone", "bonused", "outdone", "step", "seeded"))
        stored = [ph.sem(f"stored{i}") for i in range(2)]
        with nc.Block() as block:
            @block.sync
            def _(sp):
                load_weights(sp, first, [(bonus[:], column(w["faaaa"]))])
        ph.renew()
        LAG = 2
        with nc.Fori(0, B) as b:
            with nc.Block() as block:
                @block.sync
                def _(sp):
                    sp.dma_start(s0[:], w["state"][b].rearrange("(c p) d -> p c d", p=P)).then_inc(first, 16)

                    def load(c):
                        if c >= 2:
                            sp.wait_ge(outdone, c - 1)
                        for n in "rkvw":
                            sp.dma_start(src[n][c % 2][:], w["s_" + n][b, c]).then_inc(loaded[c % 2], 16)

                    load(0)
                    load(1)
                    for c in range(C):
                        sp.wait_ge(outdone, c + 1)
                        sp.dma_start(w["s_att"][b, c], o[c % 2][:]).then_inc(stored[c % 2], 16)
                        if c + 2 < C:
                            load(c + 2)
                    for half in stored:
                        sp.wait_ge(half, 16 * C // 2)

                @block.tensor
                def _(pe):
                    for c in range(C):
                        v = src["v"][c % 2]
                        pe.wait_ge(loaded[c % 2], 64 * (c // 2 + 1))
                        for d in range(HS + LAG):
                            if d < HS:
                                n = c * HS + d
                                if n >= 4:
                                    pe.wait_ge(mul, n - 3)
                                nc.tensor.matmul(vb[:, n % 4, :], k["sel"][:, d, :], v[:],
                                                 start=True, stop=True).then_inc(spread, 1)
                            if d == HS:
                                pe.wait_ge(rukdone, c + 1)
                                if c >= 1:
                                    pe.wait_ge(step, c)
                                nc.tensor.matmul(pb[:], k["head"][:], ruk[:], start=True, stop=True).then_inc(bonused, 1)
                            if d >= LAG:
                                m = c * HS + d - LAG
                                pe.wait_ge(zdone, m + 1)
                                if d == LAG and c >= 2:
                                    pe.wait_ge(outdone, c - 1)
                                nc.tensor.matmul(acc[:, c % 2, :], k["red"][:, d - LAG, :], Z[m % 3][:],
                                                 start=d == LAG, stop=d == HS + LAG - 1).then_inc(reduced, 1)

                @block.scalar
                def _(act):
                    act.wait_ge(first, 16)
                    for n in range(C * HS):
                        if n >= 3:
                            act.wait_ge(zdone, n - 2)
                            act.wait_ge(scanned, n - 2)
                        nc.scalar.activation(S[n % 3][:, 0:1], s0[:, n // HS, n % HS:n % HS + 1],
                                             ACT.Identity).then_inc(seeded, 1)

                @block.gpsimd
                def _(pool):
                    for n in range(C * HS):
                        pool.wait_ge(scanned, n + 1)
                        if n >= 3:
                            pool.wait_ge(reduced, n - 2)
                        nc.gpsimd.tensor_tensor(Z[n % 3][:], src["r"][n // HS % 2][:], S[n % 3][:, 0:T],
                                                ALU.mult).then_inc(zdone, 1)

                @block.vector
                def _(dve):
                    for c in range(C):
                        r, kk, v, dec = (src[n][c % 2] for n in "rkvw")
                        dve.wait_ge(loaded[c % 2], 64 * (c // 2 + 1))
                        for d in range(HS):
                            n = c * HS + d
                            dve.wait_ge(spread, n + 1)
                            if n >= 2:
                                dve.wait_ge(scanned, n - 1)
                            nc.vector.tensor_tensor(A[n % 2][:], kk[:], vb[:, n % 4, :], ALU.mult).then_inc(mul, 1)
                            dve.wait_ge(mul, n + 1)
                            dve.wait_ge(seeded, n + 1)
                            nc.vector.tensor_tensor_scan(S[n % 3][:, 1:], dec[:], A[n % 2][:], S[n % 3][:, 0:1],
                                                         ALU.mult, ALU.add).then_inc(scanned, 1)
                            if d == 1:
                                if c >= 1:
                                    dve.wait_ge(bonused, c)
                                nc.vector.scalar_tensor_tensor(ruk[:], r[:], bonus[:, c:c + 1], kk[:],
                                                               ALU.mult, ALU.mult).then_inc(rukdone, 1)
                        dve.wait_ge(bonused, c + 1)
                        nc.vector.tensor_tensor(bv[:], pb[:], v[:], ALU.mult).then_inc(step, 1)
                        dve.wait_ge(step, c + 1)
                        dve.wait_ge(reduced, HS * (c + 1))
                        if c >= 2:
                            dve.wait_ge(stored[c % 2], 16 * (c // 2))
                        nc.vector.tensor_tensor(o[c % 2][:], acc[:, c % 2, :], bv[:], ALU.add).then_inc(outdone, 1)
            ph.renew()


def norm_products(k, pe, group, x, squares, squared, n=T):
    group([(k["mean"][:], x[:, c, 0:n]) for c in range(C)], n=n)
    pe.wait_ge(squared, 1)
    group([(k["mean"][:], squares[:, c, 0:n]) for c in range(C)], n=n)


def norm_drains(nc, act, drain, mean, centred_x, squares, std, eps, centred, squared, n=T):
    drain(mean[:, 0:n], ACT.Identity, n=n)
    act.wait_ge(centred, 1)
    nc.scalar.activation(squares[:, :, 0:n], centred_x[:, :, 0:n], ACT.Square).then_inc(squared, 1)
    drain(std[:, 0:n], ACT.Sqrt, n=n, bias=eps[:])


def norm_steps(nc, dve, link, x, mean, centred_x, std, gamma, beta, out, drained, centred, mean_at, std_at, done, n=T):
    dve.wait_ge(drained, mean_at)
    nc.vector.tensor_tensor(centred_x[:, :, 0:n], x[:, :, 0:n], bc(mean[:, 0:n], C), ALU.subtract).then_inc(centred, 1)
    dve.wait_ge(centred, 1)
    dve.wait_ge(drained, std_at)
    link(nc.vector.reciprocal(std[:, 0:n], std[:, 0:n]))
    link(nc.vector.tensor_tensor(centred_x[:, :, 0:n], centred_x[:, :, 0:n], bc(std[:, 0:n], C), ALU.mult))
    for c in range(C):
        nc.vector.tensor_scalar(out[:, c, 0:n], centred_x[:, c, 0:n], gamma[:, c:c + 1], beta[:, c:c + 1],
                                ALU.mult, ALU.add).then_inc(done, 1)


def split_store(sp, sem, w, name, b, rows, hi, lo, cols=slice(0, T)):
    n = cols.stop - cols.start if isinstance(cols, slice) else T
    for part, half in (("hi", hi), ("lo", lo)):
        dst = w[name + part].rearrange("(b c p) t -> b p c t", b=B, p=P)[b]
        sp.dma_start(dst[:, :, cols], half[:, :, 0:n]).then_inc(sem, 16)


def rwkv_outputs(nc, w, k):
    with ExitStack() as ctx:
        ph = Phase(nc, ctx, "ffn")
        W = {n: ph.sb(n, [P, C, E]) for n in ("Wo0", "ffn_Wk", "ffn_Wr", "ffn_Wv", "Wq1")}
        vec = {n: ph.sb(n, [P, C]) for n in ("gn_w", "gn_b", "ln2_w", "ln2_b", "ffn_maa_k", "ffn_maa_r")}
        big = lambda n, dt=F32: ph.sb(n, [P, C, T], dt)
        att, gate, x, gmean, gstd, sq, o = (big(n) for n in ("att", "gate", "x", "gmean", "gstd", "sq", "o"))
        dx, kk, rr = big("dx"), big("kk"), big("rr")
        xn, prev = ph.sb("xn", [P, C, T + 1]), ph.sb("prev", [P, C])
        mean, std = ph.sb("mean", [P, T]), ph.sb("std", [P, T])
        qhi, qlo = big("qhi", F16), big("qlo", F16)
        psum = ph.ps("psum", [P, 8, T])
        loaded, product, drained, step = ph.sem("loaded"), ph.sem("product"), ph.sem("drained"), ph.sem("step")
        gcentred, gsquared, gated, residual, centred, squared, normed, mixed, relu2, done, halves, stored = (
            ph.sem(n) for n in ("gcentred", "gsquared", "gated", "residual", "centred", "squared", "normed", "mixed",
                                "relu2", "done", "halves", "stored"))
        with nc.Block() as block:
            @block.sync
            def _(sp):
                load_weights(sp, loaded, [(W[n][:], chunked(w[n])) for n in W] + [(vec[n][:], w[n]) for n in vec])
        ph.renew()
        with nc.Fori(0, B) as b:
            with nc.Block() as block:
                @block.sync
                def _(sp):
                    for dst, src in ((att, w["s_att"]), (gate, w["s_g"])):
                        sp.dma_start(dst[:], src[b].rearrange("c p t -> p c t")).then_inc(loaded, 16)
                    sp.dma_start(x[:], w["x_t"][b].rearrange("(c p) t -> p c t", p=P)).then_inc(loaded, 16)
                    sp.dma_start(prev[:], w["prev0"][b]).then_inc(loaded, 16)
                    sp.wait_ge(done, 1)
                    sp.dma_start(w["x1"][b].rearrange("(c p) t -> p c t", p=P), x[:]).then_inc(stored, 16)
                    sp.wait_ge(halves, 2)
                    split_store(sp, stored, w, "q1", b, E, qhi, qlo)
                    sp.wait_ge(stored, 48)

                @block.tensor
                def _(pe):
                    group = Banks(nc, pe, psum, product, drained)

                    def project(weight, src):
                        for o_ in range(C):
                            group([(W[weight][:, c, o_ * P:(o_ + 1) * P], src[:, c, 0:T]) for c in range(C)])

                    pe.wait_ge(loaded, 64)
                    for c in range(C):
                        group([(k["headmean"][:], att[:, c, :])])
                    pe.wait_ge(gsquared, 1)
                    for c in range(C):
                        group([(k["headmean"][:], sq[:, c, :])])
                    pe.wait_ge(gated, 1)
                    project("Wo0", att)
                    pe.wait_ge(residual, 1)
                    norm_products(k, pe, group, x, sq, squared)
                    pe.wait_ge(mixed, C)
                    project("ffn_Wk", gmean)
                    pe.wait_ge(mixed, 2 * C)
                    project("ffn_Wr", gstd)
                    pe.wait_ge(relu2, 1)
                    project("ffn_Wv", kk)
                    pe.wait_ge(done, 1)
                    project("Wq1", x)

                @block.scalar
                def _(act):
                    drain = Drains(nc, act, psum, product, drained)
                    for c in range(C):
                        drain(gmean[:, c, :], ACT.Identity)
                    act.wait_ge(gcentred, 1)
                    nc.scalar.activation(sq[:], att[:], ACT.Square).then_inc(gsquared, 1)
                    for c in range(C):
                        drain(gstd[:, c, :], ACT.Sqrt, bias=k["eps5"][:])
                    for c in range(C):
                        drain(o[:, c, :], ACT.Identity)
                    norm_drains(nc, act, drain, mean, o, sq, std, k["eps5"], centred, squared)
                    for c in range(C):
                        drain(kk[:, c, :], ACT.Relu)
                    for c in range(C):
                        drain(rr[:, c, :], ACT.Sigmoid)
                    for c in range(C):
                        drain(o[:, c, :], ACT.Identity)
                    for c in range(C):
                        drain(sq[:, c, :], ACT.Identity, scale=32 ** -0.5)

                @block.vector
                def _(dve):
                    link = Chain(dve, step)
                    dve.wait_ge(loaded, 64)
                    link(nc.vector.tensor_copy(xn[:, :, 0], prev[:]))
                    dve.wait_ge(drained, C)
                    nc.vector.tensor_tensor(att[:], att[:], gmean[:], ALU.subtract).then_inc(gcentred, 1)
                    dve.wait_ge(gcentred, 1)
                    dve.wait_ge(drained, 2 * C)
                    link(nc.vector.reciprocal(gstd[:], gstd[:]))
                    link(nc.vector.tensor_tensor(att[:], att[:], gstd[:], ALU.mult))
                    for c in range(C):
                        link(nc.vector.tensor_scalar(att[:, c, :], att[:, c, :], vec["gn_w"][:, c:c + 1],
                                                     vec["gn_b"][:, c:c + 1], ALU.mult, ALU.add))
                    nc.vector.tensor_tensor(att[:], att[:], gate[:], ALU.mult).then_inc(gated, 1)
                    dve.wait_ge(drained, 3 * C)
                    nc.vector.tensor_tensor(x[:], x[:], o[:], ALU.add).then_inc(residual, 1)
                    dve.wait_ge(residual, 1)
                    norm_steps(nc, dve, link, x, mean, o, std, vec["ln2_w"], vec["ln2_b"], xn[:, :, 1:], drained,
                               centred, 3 * C + 1, 3 * C + 2, normed)
                    dve.wait_ge(normed, C)
                    link(nc.vector.tensor_tensor(dx[:], xn[:, :, 0:T], xn[:, :, 1:], ALU.subtract))
                    for m, dst in (("ffn_maa_k", gmean), ("ffn_maa_r", gstd)):
                        for c in range(C):
                            nc.vector.scalar_tensor_tensor(dst[:, c, :], dx[:, c, :], vec[m][:, c:c + 1],
                                                           xn[:, c, 1:], ALU.mult, ALU.add).then_inc(mixed, 1)
                    dve.wait_ge(drained, 4 * C + 2)
                    nc.vector.tensor_tensor(kk[:], kk[:], kk[:], ALU.mult).then_inc(relu2, 1)
                    dve.wait_ge(drained, 6 * C + 2)
                    link(nc.vector.tensor_tensor(rr[:], rr[:], o[:], ALU.mult))
                    nc.vector.tensor_tensor(x[:], x[:], rr[:], ALU.add).then_inc(done, 1)
                    dve.wait_ge(drained, 7 * C + 2)
                    nc.vector.tensor_copy(qhi[:], sq[:]).then_inc(halves, 1)
                    dve.wait_ge(halves, 1)
                    nc.vector.tensor_tensor(qlo[:], sq[:], qhi[:], ALU.subtract).then_inc(halves, 1)
            ph.renew()


def context_keys(nc, w, k):
    with ExitStack() as ctx:
        ph = Phase(nc, ctx, "ctx")
        W = {n: ph.sb(n, [P, C, m]) for n, m in (("Wk1", E), ("Wv1", E), ("Wk2", P), ("Wv2", P), ("k_w3", E), ("v_w3", E))}
        vec = {"ln_gamma1": ph.sb("gamma", [P, C]), "ln_beta1": ph.sb("beta", [P, C]), "bk2": ph.sb("bk2", [P, 1]),
               "k_b3": ph.sb("bk3", [P, C])}
        row = {"bv2": ph.sb("bv2", [1, P]), "v_b3": ph.sb("bv3", [1, E])}
        x, xc, sq, a = (ph.sb(n, [P, C, KT]) for n in ("x", "xc", "sq", "a"))
        mean, std = ph.sb("mean", [P, KT]), ph.sb("std", [P, KT])
        kf = ph.sb("kf", [P, C, KT])
        hi, lo = ([ph.sb(f"{n}{i}", [P, C, KT], F16) for i in range(2)] for n in ("hi", "lo"))
        k2f, k2hi, k2lo = ph.sb("k2f", [P, 1, KT]), ph.sb("k2hi", [P, 1, KT], F16), ph.sb("k2lo", [P, 1, KT], F16)
        v = [ph.sb(f"v{i}", [P, E]) for i in range(4)]
        v2 = [ph.sb(f"v2{i}", [P, P]) for i in range(4)]
        psum = ph.ps("psum", [P, 8, KT])
        loaded, product, drained, step = ph.sem("loaded"), ph.sem("product"), ph.sem("drained"), ph.sem("step")
        centred, squared, normed, halves, stored = (
            ph.sem(n) for n in ("centred", "squared", "normed", "halves", "stored"))
        vstored = [ph.sem(f"vstored{i}") for i in range(4)]
        with nc.Block() as block:
            @block.sync
            def _(sp):
                load_weights(sp, loaded, [(W[n][:], chunked(w[n])) for n in W] + [(vec[n][:], w[n]) for n in vec]
                             + [(row[n][:], w[n].unsqueeze(0)) for n in row])
        ph.renew()

        def tile(b, t0, n):
            tt = -(-n // P)
            width = [min(P, n - P * i) for i in range(tt)]
            k2_end = 2
            v2_end = k2_end + tt
            k3_end = v2_end + C
            v3_end = k3_end + tt
            std_end = v3_end + 1
            k1_end = std_end + C
            cols = bass.ds(t0, n)
            with nc.Block() as block:
                @block.sync
                def _(sp):
                    sp.dma_start(x[:, :, 0:n], w["ctx_t"][b].rearrange("(c p) t -> p c t", p=P)[:, :, cols]).then_inc(loaded, 16)

                    def halves_out(count, name, hi_, lo_):
                        sp.wait_ge(halves, count)
                        for part, half in (("hi", hi_), ("lo", lo_)):
                            dst = w[name + part].rearrange("(b c p) t -> b p c t", b=B, p=P)[b]
                            sp.dma_start(dst[:, :, cols], half[:, :, 0:n]).then_inc(stored, 16)

                    def values_out(name, end):
                        for i, m in enumerate(width):
                            sp.wait_ge(drained, end - tt + i + 1)
                            if name == "v2":
                                dst = w["v2"].rearrange("(b g) s d -> b s g d", b=B)[b, bass.ds(t0 + i * P, m)]
                                sp.dma_start(dst, v2[i][0:m].rearrange("p (g d) -> p g d", d=HS)).then_inc(stored, 16)
                            else:
                                dst = w[name].rearrange("(b g) s d -> b s g d", b=B)[b, bass.ds(t0 + i * P, m)]
                                sp.dma_start(dst, v[i][0:m].rearrange("p (g d) -> p g d", g=QUAD)).then_inc(vstored[i], 16)

                    values_out("v2", v2_end)
                    halves_out(2, "k2", k2hi, k2lo)
                    values_out("v3", v3_end)
                    halves_out(4, "k3", hi[0], lo[0])
                    values_out("v1", k1_end + tt)
                    halves_out(6, "k1", hi[1], lo[1])
                    sp.wait_ge(stored, 16 * (tt + 6))
                    for i in range(tt):
                        sp.wait_ge(vstored[i], 32)

                @block.tensor
                def _(pe):
                    group = Banks(nc, pe, psum, product, drained)

                    def keys(weight, src, chunks=C):
                        for o in range(chunks):
                            group([(W[weight][:, c, o * P:(o + 1) * P], src[:, c, 0:n]) for c in range(C)], n=n)

                    def values(weight, src, bias=None, m=E):
                        for i, wd in enumerate(width):
                            pairs = [(src[:, c, i * P:i * P + wd], W[weight][:, c, :]) for c in range(C)]
                            if bias is not None:
                                pairs.append((k["ones"][0:1, 0:wd], bias[:]))
                            group(pairs, m=wd, n=m)

                    pe.wait_ge(loaded, 16)
                    group([(k["mean"][:], x[:, c, 0:n]) for c in range(C)], n=n)
                    keys("Wk2", x, 1)
                    values("Wv2", x, row["bv2"], P)
                    keys("k_w3", x)
                    values("v_w3", x, row["v_b3"])
                    pe.wait_ge(squared, 1)
                    group([(k["mean"][:], sq[:, c, 0:n]) for c in range(C)], n=n)
                    pe.wait_ge(normed, C)
                    keys("Wk1", a)
                    values("Wv1", a)

                @block.scalar
                def _(act):
                    drain = Drains(nc, act, psum, product, drained)
                    drain(mean[:, 0:n], ACT.Identity, n=n)
                    drain(k2f[:, 0, 0:n], ACT.Identity, n=n, bias=vec["bk2"][:])
                    for i, m in enumerate(width):
                        drain(v2[i][0:m], ACT.Identity, m=m, n=P)
                    act.wait_ge(centred, 1)
                    nc.scalar.activation(sq[:, :, 0:n], xc[:, :, 0:n], ACT.Square).then_inc(squared, 1)
                    for o in range(C):
                        drain(kf[:, o, 0:n], ACT.Identity, n=n, bias=vec["k_b3"][:, o:o + 1])
                    for i, m in enumerate(width):
                        drain(v[i][0:m], ACT.Identity, m=m, n=E)
                    drain(std[:, 0:n], ACT.Sqrt, n=n, bias=k["eps5"][:])
                    act.wait_ge(halves, 4)
                    for o in range(C):
                        drain(kf[:, o, 0:n], ACT.Identity, n=n)
                    for i, m in enumerate(width):
                        act.wait_ge(vstored[i], 16)
                        drain(v[i][0:m], ACT.Identity, m=m, n=E)

                @block.vector
                def _(dve):
                    link = Chain(dve, step)

                    def split(end, full, hi_, lo_, count):
                        dve.wait_ge(drained, end)
                        nc.vector.tensor_copy(hi_[:, :, 0:n], full[:, :, 0:n]).then_inc(halves, 1)
                        dve.wait_ge(halves, count)
                        nc.vector.tensor_tensor(lo_[:, :, 0:n], full[:, :, 0:n], hi_[:, :, 0:n],
                                                ALU.subtract).then_inc(halves, 1)

                    dve.wait_ge(loaded, 16)
                    dve.wait_ge(drained, 1)
                    nc.vector.tensor_tensor(xc[:, :, 0:n], x[:, :, 0:n], bc(mean[:, 0:n], C), ALU.subtract).then_inc(centred, 1)
                    split(2, k2f, k2hi, k2lo, 1)
                    split(k3_end, kf, hi[0], lo[0], 3)
                    dve.wait_ge(drained, std_end)
                    dve.wait_ge(centred, 1)
                    link(nc.vector.reciprocal(std[:, 0:n], std[:, 0:n]))
                    link(nc.vector.tensor_tensor(xc[:, :, 0:n], xc[:, :, 0:n], bc(std[:, 0:n], C), ALU.mult))
                    for c in range(C):
                        nc.vector.tensor_scalar(a[:, c, 0:n], xc[:, c, 0:n], vec["ln_gamma1"][:, c:c + 1],
                                                vec["ln_beta1"][:, c:c + 1], ALU.mult, ALU.add).then_inc(normed, 1)
                    split(k1_end, kf, hi[1], lo[1], 5)
            ph.renew()

        with nc.Fori(0, B) as b:
            with nc.Fori(0, FULL) as i:
                tile(b, i * KT, KT)
            tile(b, FULL * KT, TAIL)


def attention(nc, w, k, layer, add=False):
    dh = 16 if layer == 2 else 32
    latents = T if layer == 3 else 0
    NK = latents + S2
    NT = -(-NK // P)
    quads = E // dh // QUAD
    KH = 1 if layer == 2 else QUAD
    HALF = [("hi", "hi"), ("hi", "lo"), ("lo", "hi")] + ([("lo", "lo")] if dh == 16 else [])
    STACK = len(HALF) * dh
    WITH_ONES = layer == 2
    BANKS = 1 if WITH_ONES else 2
    RING1, RING2 = (4, 3) if WITH_ONES else (3, 3)
    MROW = P - 1
    PIECES = -(-NK // T)
    PIECE = -(-NK // PIECES)
    UNITS = QUAD * C * PIECES
    PER = -(-(UNITS + 1) // (NT - 2))
    END1 = UNITS // PER
    NB = 3
    OUTS = QUAD if dh < 32 else 1
    with ExitStack() as ctx:
        ph = Phase(nc, ctx, f"att{layer}{'m' if add else ''}")
        VC = 32 if WITH_ONES else P
        Q = [ph.sb(f"q{i}", [P, QUAD, T], F16) for i in range(NB)]
        K = [ph.sb(f"k{i}", [P, KH, NK], F16) for i in range(NB)]
        V = [ph.sb(f"v{i}", [P, NT, VC]) for i in range(NB)]
        prob = [ph.sb(f"prob{i}", [P, QUAD, T]) for i in range(2)]
        part = ph.sb("part", [P, QUAD * C, PIECES])
        top = ph.sb("top", [P, QUAD * C])
        topT = ph.sb("topT", [QUAD * C, P], F32 if add else F16)
        sums_sb = ph.sb("sums_sb", [P, BANKS, T])
        recip, spread, out = ph.sb("recip", [P, T]), ph.sb("spread", [P, T]), ph.sb("out", [P, T])
        scores1 = ph.ps("scores1", [P, RING1, T])
        scores2 = ph.ps("scores2", [P, RING2, T])
        sums = ph.ps("sums", [P, BANKS, T])
        if add:
            mask = ph.sb("mask", [P, C, S2])
            mask_t = ph.sb("mask_t", [P, NT, T])
            junk = ph.sb("junk", [P, RING1, T], mybir.dt.bfloat16)
            summed = ph.sb("summed", [P, RING2, T])
            maxima = [ph.sb(f"maxima{i}", [P, QUAD, T]) for i in range(NB)]
        added = ph.sem("added")
        fixed, loaded = ph.sem("fixed"), [ph.sem(f"loaded{i}") for i in range(NB)]
        scored, reduced, maxed, turned, rounded, topout, topsent, cleared = (
            ph.sem(n) for n in ("scored", "reduced", "maxed", "turned", "rounded", "topout", "topsent", "cleared"))
        shifted, masked, exped, mixdone, evacuated, normed, stored, step = (
            ph.sem(n) for n in ("shifted", "masked", "exped", "mixdone", "evacuated", "normed", "stored", "step"))

        def once(b):
            with nc.Block() as block:
                @block.vector
                def _(dve):
                    for i in range(NB):
                        nc.vector.memset(Q[i][:], 0.0).then_inc(cleared, 1)
                        nc.vector.memset(K[i][:], 0.0).then_inc(cleared, 1)

                @block.sync
                def _(sp):
                    sp.wait_ge(cleared, 2 * NB)
                    moves = []
                    for i in range(NB):
                        moves.append((K[i][MROW:MROW + 1], w["c_k"][0:KH * NK].rearrange("(o h s) -> o h s", o=1, h=KH)))
                        moves.append((Q[i][STACK:STACK + 1], w["c_q"].rearrange("(o h s) -> o h s", o=1, h=QUAD)))
                        if WITH_ONES:
                            moves.append((V[i][:, :, HS:2 * HS], w["c_ones"][:, 0:NT]))
                    if add:
                        full = NT - 1
                        moves.append((mask[:], w["mask2"][b].rearrange("(c p) s -> p c s", p=P)))
                        moves.append((mask_t[:, 0:full], w["mask2_t"][b][0:full * P].rearrange("(c p) t -> p c t", p=P)))
                        moves.append((mask_t[0:NK - full * P, full], w["mask2_t"][b][full * P:NK]))
                    load_weights(sp, fixed, moves)
            ph.renew()

        LOADS = 2 * len(HALF) + 2 + (0 if layer == 2 else 1) + (4 if latents else 0)

        def load(sp, j, i):
            def go(dst, src):
                sp.dma_start(dst, src).then_inc(loaded[i], 16)

            rows = bass.ds(j * (QUAD * dh), QUAD * dh)
            krows = bass.ds(j * (KH * dh), KH * dh)
            for n, (qp, kp) in enumerate(HALF):
                r = slice(n * dh, (n + 1) * dh)
                go(Q[i][r], w[f"q{layer}{qp}"][rows].rearrange("(h d) t -> d h t", d=dh))
                go(K[i][r, :, latents:], w[f"k{layer}{kp}"][krows].rearrange("(h d) t -> d h t", d=dh))
                if latents:
                    go(K[i][r, :, 0:latents], w[f"kx{kp}"][krows].rearrange("(h d) t -> d h t", d=dh))
            lt, full = latents // P, S2 // P
            if latents:
                go(V[i][:, 0:lt], w["vx"][j].rearrange("(c p) d -> p c d", p=P))
            vc, v = HS if WITH_ONES else VC, w[f"v{layer}"]
            go(V[i][:, lt:lt + full, 0:vc], v[j, 0:full * P].rearrange("(c p) d -> p c d", p=P))
            go(V[i][0:S2 - full * P, lt + full, 0:vc], v[j, full * P:S2])
            if layer != 2:
                km = w[f"km{layer}"].rearrange("b g s -> (b g) s")[j]
                go(K[i][STACK:STACK + 1, :, latents:], km.unsqueeze(0).unsqueeze(0).broadcast_to([1, KH, S2]))

        def run(j, steps, left=None):
            left = left if left is not None else steps + 2
            plan = [(None, (j, 0), (j + 1, 1))] if steps == 0 else [
                ((j + s, s % NB), (j + s + 1, (s + 1) % NB) if s + 1 < left else None,
                 (j + s + 2, (s + 2) % NB) if s + 2 < left else None) for s in range(steps)]
            fresh = {}
            for s, (_, _, ld) in enumerate(plan):
                if ld:
                    fresh[ld[1]] = s
            if steps == 0:
                fresh[0] = 0
            n1 = sum(1 for _, p1, _ in plan if p1)
            with nc.Block() as block:
                @block.sync
                def _(sp):
                    seen1 = 0
                    if steps == 0:
                        load(sp, j, 0)
                    for s, (p2, p1, ld) in enumerate(plan):
                        if ld:
                            if s:
                                sp.wait_ge(mixdone, NT * s)
                            load(sp, *ld)
                        if s:
                            sp.wait_ge(normed, s)
                            rows = w[f"o{layer}"][bass.ds(plan[s - 1][0][0] * (QUAD * dh), QUAD * dh)]
                            for h in range(OUTS):
                                m = P if OUTS == 1 else dh
                                sp.dma_start(rows[h * m:(h + 1) * m], out[32 * h:32 * h + m]).then_inc(stored, 16)
                        if p1:
                            seen1 += 1
                            sp.wait_ge(rounded, seen1)
                            tops = w["tops_f32" if add else "tops"]
                            sp.dma_start(tops, topT[:]).then_inc(topout, 16)
                            sp.wait_ge(topout, 16 * seen1)
                            row = tops.rearrange("(o h c) t -> o h (c t)", o=1, h=QUAD)
                            sp.dma_start(maxima[p1[1]][:] if add else Q[p1[1]][MROW:MROW + 1],
                                         row.broadcast_to([P, QUAD, T]) if add else row).then_inc(topsent, 16)
                    if steps:
                        sp.wait_ge(normed, steps)
                        rows = w[f"o{layer}"][bass.ds(plan[-1][0][0] * (QUAD * dh), QUAD * dh)]
                        for h in range(OUTS):
                            m = P if OUTS == 1 else dh
                            sp.dma_start(rows[h * m:(h + 1) * m], out[32 * h:32 * h + m]).then_inc(stored, 16)
                        sp.wait_ge(stored, 16 * steps * OUTS)
                    if n1:
                        sp.wait_ge(topsent, 16 * n1)
                    for i in fresh:
                        sp.wait_ge(loaded[i], 16 * LOADS)

                @block.tensor
                def _(pe):
                    seen1 = 0
                    for s, (p2, p1, _) in enumerate(plan):
                        def pass1():
                            i = p1[1]
                            if i in fresh and (steps == 0 or fresh[i] < s):
                                pe.wait_ge(loaded[i], 16 * LOADS)
                            for u in range(UNITS + 1):
                                n = seen1 * (UNITS + 1) + u
                                if n >= RING1:
                                    pe.wait_ge(reduced, n - RING1 + 1)
                                if u == UNITS:
                                    pe.wait_ge(maxed, seen1 + 1)
                                    nc.tensor.transpose(scores1[0:QUAD * C, n % RING1, 0:P], top[:],
                                                        k["ident"][:]).then_inc(turned, 1)
                                else:
                                    h, c, piece = u // (C * PIECES), u // PIECES % C, u % PIECES
                                    k0, k1 = piece * PIECE, min(NK, (piece + 1) * PIECE)
                                    nc.tensor.matmul(scores1[:, n % RING1, 0:k1 - k0], Q[i][0:MROW, h, c * P:(c + 1) * P],
                                                     K[i][0:MROW, 0 if KH == 1 else h, k0:k1],
                                                     start=True, stop=True).then_inc(scored, 1)
                                yield

                        one = pass1() if p1 else iter(())
                        if p2:
                            i = p2[1]
                            used = MROW if add else MROW + 1
                            if s:
                                pe.wait_ge(topsent, 16 * s)

                            def shift(kt, h):
                                n = (s * NT + kt) * QUAD + h
                                kw = min(P, NK - kt * P)
                                if n >= RING2:
                                    pe.wait_ge(masked if add else exped, n - RING2 + 1)
                                nc.tensor.matmul(scores2[0:kw, n % RING2, :],
                                                 K[i][0:used, 0 if KH == 1 else h, kt * P:kt * P + kw],
                                                 Q[i][0:used, h, :], start=True, stop=True).then_inc(shifted, 1)

                            def mix(t, bank):
                                kw = min(P, NK - t * P)
                                pe.wait_ge(exped, (s * NT + t + 1) * QUAD)
                                if t == 0 and s:
                                    pe.wait_ge(evacuated, s)
                                pr = prob[(s * NT + t) % 2]
                                for h in range(QUAD):
                                    lhsT = k["ones"][0:kw, 0:32] if bank else (
                                        V[i][0:kw, t, 0:32] if KH == 1 else V[i][0:kw, t, 32 * h:32 * h + 32])
                                    ins = nc.tensor.matmul(sums[32 * h:32 * h + 32, bank, :], lhsT, pr[0:kw, h, :],
                                                           start=t == 0, stop=t == NT - 1,
                                                           tile_position=(0, 32 * h))
                                if bank == BANKS - 1:
                                    ins.then_inc(mixdone, 1)

                            for kt in range(NT + 1):
                                budget = PER if kt < NT else 0
                                for h in range(QUAD):
                                    if kt < NT:
                                        shift(kt, h)
                                    if budget:
                                        next(one, None)
                                        budget -= 1
                                if kt >= 1:
                                    mix(kt - 1, 0)
                                if budget:
                                    next(one, None)
                                    budget -= 1
                                if kt >= 1 and BANKS == 2:
                                    mix(kt - 1, 1)
                                for _ in range(budget):
                                    next(one, None)
                        for _ in one:
                            pass
                        if p1:
                            seen1 += 1

                @block.scalar
                def _(act):
                    for s, (p2, p1, _) in enumerate(plan):
                        def top_row():
                            act.wait_ge(turned, s + 1)
                            if s:
                                act.wait_ge(topout, 16 * s)
                            slot = (s * (UNITS + 1) + UNITS) % RING1
                            nc.scalar.activation(topT[:], scores1[0:QUAD * C, slot, 0:P], ACT.Identity).then_inc(rounded, 1)

                        for kt in range(NT if p2 else 0):
                            g = s * NT + kt
                            if g >= 2:
                                act.wait_ge(mixdone, g - 1)
                            kw = min(P, NK - kt * P)
                            for h in range(QUAD):
                                n = g * QUAD + h
                                act.wait_ge(masked if add else shifted, n + 1)
                                src = summed if add else scores2
                                nc.scalar.activation(prob[g % 2][0:kw, h, :], src[0:kw, n % RING2, :], ACT.Exp).then_inc(exped, 1)
                            if p1 and kt == END1:
                                top_row()
                        if not p2:
                            top_row()

                @block.vector
                def _(dve):
                    link = Chain(dve, step)

                    def normalise(s):
                        if WITH_ONES:
                            swap = [(m + HS) % 32 for m in range(32)]
                            link(nc.vector.stream_shuffle(spread[:], sums_sb[:, 0, :], swap))
                            yield
                        for q in range(C):
                            cols = slice(q * P, (q + 1) * P)
                            link(nc.vector.reciprocal(recip[:, cols], spread[:, cols] if WITH_ONES else sums_sb[:, 1, cols]))
                            yield
                        if s:
                            dve.wait_ge(stored, 16 * s * OUTS)
                        nc.vector.tensor_tensor(out[:], sums_sb[:, 0, :], recip[:], ALU.mult).then_inc(normed, 1)

                    pending = iter(())
                    for s, (p2, p1, _) in enumerate(plan):
                        def pass1():
                            for u in range(UNITS):
                                h, c, piece = u // (C * PIECES), u // PIECES % C, u % PIECES
                                n = s * (UNITS + 1) + u
                                k0, k1 = piece * PIECE, min(NK, (piece + 1) * PIECE)
                                dve.wait_ge(scored, s * UNITS + u + 1)
                                dst, src = part[:, h * C + c, piece:piece + 1], scores1[:, n % RING1, 0:k1 - k0]
                                if add:
                                    if n >= RING1:
                                        dve.wait_ge(reduced, n - RING1 + 1)
                                    nc.vector.tensor_tensor_reduce(
                                        out=junk[:, n % RING1, 0:k1 - k0], in0=src, in1=mask[:, c, k0:k1], scale=1.0,
                                        scalar=-3.0e38, op0=ALU.add, op1=ALU.max, accum_out=dst).then_inc(reduced, 1)
                                else:
                                    nc.vector.reduce_max(dst, src, AX.X).then_inc(reduced, 1)
                                if u % 3 == 2:
                                    next(pending, None)
                                yield
                            dve.wait_ge(reduced, s * (UNITS + 1) + UNITS)
                            nc.vector.reduce_max(top[:], part[:], AX.X).then_inc(maxed, 1)
                            yield
                            dve.wait_ge(rounded, s + 1)
                            dve.wait_ge(maxed, s + 1)
                            nc.vector.memset(part[:], 0.0).then_inc(reduced, 1)
                            yield

                        one = pass1() if p1 else iter(())
                        if p2 and add:
                            units = UNITS + 1 if p1 else 0
                            if s:
                                dve.wait_ge(topsent, 16 * s)
                            for kt in range(NT):
                                kw = min(P, NK - kt * P)
                                budget = min(PER, units)
                                units -= budget
                                for h in range(QUAD):
                                    n = (s * NT + kt) * QUAD + h
                                    dve.wait_ge(shifted, n + 1)
                                    if n >= RING2:
                                        dve.wait_ge(exped, n - RING2 + 1)
                                    nc.vector.tensor_tensor(summed[0:kw, n % RING2, :], scores2[0:kw, n % RING2, :],
                                                            mask_t[0:kw, kt, :], ALU.add).then_inc(added, 1)
                                    dve.wait_ge(added, n + 1)
                                    nc.vector.tensor_tensor(summed[0:kw, n % RING2, :], summed[0:kw, n % RING2, :],
                                                            maxima[p2[1]][0:kw, h, :], ALU.subtract).then_inc(masked, 1)
                                    if budget:
                                        next(one, None)
                                        budget -= 1
                                for _ in range(budget):
                                    next(one, None)
                        for _ in one:
                            pass
                        for _ in pending:
                            pass
                        if p2:
                            dve.wait_ge(mixdone, NT * (s + 1))
                            if s:
                                dve.wait_ge(normed, s)
                            nc.vector.tensor_copy(sums_sb[:], sums[:]).then_inc(evacuated, 1)
                            dve.wait_ge(evacuated, s + 1)
                            pending = normalise(s)
                    for _ in pending:
                        pass
            ph.renew()

        def whole(first, count):
            bodies = (count - 2) // NB
            run(first, 0)
            with nc.Fori(0, bodies) as i:
                run(first + i * NB, NB)
            rest = count - bodies * NB
            run(first + bodies * NB, rest, rest)

        if add:
            with nc.Fori(0, B) as b:
                once(b)
                whole(b * quads, quads)
        else:
            once(None)
            whole(0, B * quads)


def masks_at_all(nc, w, k):
    with ExitStack() as ctx:
        ph = Phase(nc, ctx, "anymask")
        m = [ph.sb(f"m{i}", [P, C, S2]) for i in range(2)]
        ends = ph.sb("ends", [P, 2 * B])
        odd, count = ph.sb("odd", [P, 2 * B]), ph.sb("count", [P, 2 * B])
        seen, flag = ph.sb("seen", [P, 1]), ph.sb("flag", [P, 1], I32)
        psum = ph.ps("psum", [P, T])
        loaded = [ph.sem(f"loaded{i}") for i in range(2)]
        reduced, marked, summed, made, step, stored = (
            ph.sem(n) for n in ("reduced", "marked", "summed", "made", "step", "stored"))
        with nc.Block() as block:
            @block.sync
            def _(sp):
                for b in range(B):
                    if b >= 2:
                        sp.wait_ge(reduced, 2 * (b - 1))
                    sp.dma_start(m[b % 2][:], w["mask2"][b].rearrange("(c p) s -> p c s", p=P)).then_inc(loaded[b % 2], 16)
                sp.wait_ge(made, 1)
                sp.dma_start(w["anymask"], flag[0:1, :]).then_inc(stored, 16)
                sp.wait_ge(stored, 16)

            @block.tensor
            def _(pe):
                pe.wait_ge(marked, 1)
                nc.tensor.matmul(psum[:, 0:2 * B], k["ones"][:], odd[:], start=True, stop=True).then_inc(summed, 1)

            @block.vector
            def _(dve):
                link = Chain(dve, step)
                for b in range(B):
                    dve.wait_ge(loaded[b % 2], 16 * (b // 2 + 1))
                    flat = m[b % 2][:].rearrange("p c s -> p (c s)")
                    nc.vector.reduce_max(ends[:, 2 * b:2 * b + 1], flat, AX.X).then_inc(reduced, 1)
                    nc.vector.tensor_reduce(ends[:, 2 * b + 1:2 * b + 2], flat, AX.X, ALU.min).then_inc(reduced, 1)
                dve.wait_ge(reduced, 2 * B)
                nc.vector.tensor_scalar(odd[:], ends[:], 0.0, None, ALU.not_equal).then_inc(marked, 1)
                dve.wait_ge(summed, 1)
                link(nc.vector.tensor_copy(count[:], psum[:, 0:2 * B]))
                link(nc.vector.reduce_max(seen[:], count[:], AX.X))
                link(nc.vector.tensor_scalar(seen[:], seen[:], 0.0, None, ALU.not_equal))
                nc.vector.tensor_copy(flag[:], seen[:]).then_inc(made, 1)
        ph.renew()
    return nc.values_load(w["anymask"], min_val=0, max_val=1)


def attention2(nc, w, k):
    some = masks_at_all(nc, w, k)
    with nc.If(some == 0):
        attention(nc, w, k, 2)
    with nc.Else():
        attention(nc, w, k, 2, add=True)


def scratch(nc, w):
    def dram(name, shape, dt=F32):
        w[name] = nc.dram_tensor(name, shape, dt).ap()

    for n in "rkvwg":
        dram("s_" + n, [B, C, P, T])
    dram("s_att", [B, C, P, T])
    for n in ("km1", "km3"):
        dram(n, [B, QUAD, S2], F16)
    for n in ("x1", "x2", "x3"):
        dram(n, [B, E, T])
    for n in ("o1", "o2", "o3"):
        dram(n, [B * E, T])
    for j in (1, 2, 3):
        for part in ("hi", "lo"):
            dram(f"q{j}{part}", [B * E, T], F16)
    for j, rows in ((1, E), (2, P), (3, E)):
        for part in ("hi", "lo"):
            dram(f"k{j}{part}", [B * rows, S2], F16)
    for part in ("hi", "lo"):
        dram(f"kx{part}", [B * E, T], F16)
    dram("v1", [B * QUAD, S2, P])
    dram("v2", [B * 8, S2, HS])
    dram("v3", [B * QUAD, S2, P])
    dram("vx", [B * QUAD, T, P])
    dram("tops", [QUAD * C, P], F16)
    dram("anymask", [1, 1], I32)
    dram("tops_f32", [QUAD * C, P])


def rows_of(ap, b):
    if len(ap.shape) == 3:
        return ap[b].rearrange("(c p) t -> p c t", p=P)
    return ap.rearrange("(b c p) t -> b p c t", b=B, p=P)[b]


def between_1_2(nc, w, k):
    with ExitStack() as ctx:
        ph = Phase(nc, ctx, "mid1")
        W = {n: ph.sb(n, [P, C, E]) for n in ("Wo1", "Wq2")}
        bq, gate = ph.sb("bq", [P, C]), ph.sb("gate", [P, 1])
        o, x, y, q = (ph.sb(n, [P, C, T]) for n in ("o", "x", "y", "q"))
        qhi, qlo = ph.sb("qhi", [P, C, T], F16), ph.sb("qlo", [P, C, T], F16)
        psum = ph.ps("psum", [P, 8, T])
        loaded, product, drained, step = ph.sem("loaded"), ph.sem("product"), ph.sem("drained"), ph.sem("step")
        done, halves, stored = ph.sem("done"), ph.sem("halves"), ph.sem("stored")
        with nc.Block() as block:
            @block.sync
            def _(sp):
                load_weights(sp, loaded, [(W[n][:], chunked(w[n])) for n in W] + [
                    (bq[:], w["bq2"]), (gate[:], w["gate1"].unsqueeze(0).broadcast_to([P, 1]))])

            @block.scalar
            def _(act):
                act.wait_ge(loaded, 64)
                nc.scalar.activation(gate[:], gate[:], ACT.Tanh).then_inc(step, 1)
                nc.scalar.activation(bq[:], bq[:], ACT.Identity, scale=HS ** -0.5).then_inc(step, 1)
        ph.renew()
        with nc.Fori(0, B) as b:
            with nc.Block() as block:
                @block.sync
                def _(sp):
                    sp.dma_start(o[:], rows_of(w["o1"], b)).then_inc(loaded, 16)
                    sp.dma_start(x[:], rows_of(w["x1"], b)).then_inc(loaded, 16)
                    sp.wait_ge(done, 1)
                    sp.dma_start(rows_of(w["x2"], b), x[:]).then_inc(stored, 16)
                    sp.wait_ge(halves, 2)
                    split_store(sp, stored, w, "q2", b, E, qhi, qlo)
                    sp.wait_ge(stored, 48)

                @block.tensor
                def _(pe):
                    group = Banks(nc, pe, psum, product, drained)
                    pe.wait_ge(loaded, 32)
                    for i in range(C):
                        group([(W["Wo1"][:, c, i * P:(i + 1) * P], o[:, c, :]) for c in range(C)])
                    pe.wait_ge(done, 1)
                    for i in range(C):
                        group([(W["Wq2"][:, c, i * P:(i + 1) * P], x[:, c, :]) for c in range(C)])

                @block.scalar
                def _(act):
                    drain = Drains(nc, act, psum, product, drained)
                    for c in range(C):
                        drain(y[:, c, :], ACT.Identity, scale=gate[:])
                    for c in range(C):
                        drain(q[:, c, :], ACT.Identity, scale=HS ** -0.5, bias=bq[:, c:c + 1])

                @block.vector
                def _(dve):
                    dve.wait_ge(loaded, 32)
                    dve.wait_ge(drained, C)
                    nc.vector.tensor_tensor(x[:], x[:], y[:], ALU.add).then_inc(done, 1)
                    dve.wait_ge(drained, 2 * C)
                    nc.vector.tensor_copy(qhi[:], q[:]).then_inc(halves, 1)
                    dve.wait_ge(halves, 1)
                    nc.vector.tensor_tensor(qlo[:], q[:], qhi[:], ALU.subtract).then_inc(halves, 1)
            ph.renew()


def between_2_3(nc, w, k):
    with ExitStack() as ctx:
        ph = Phase(nc, ctx, "mid2")
        W = {n: ph.sb(n, [P, C, E]) for n in ("Wo2", "q_w3", "k_w3", "v_w3")}
        vec = {n: ph.sb(n, [P, C]) for n in ("bo2", "gamma2", "beta2", "q_b3", "k_b3")}
        bv = ph.sb("bv", [1, E])
        o, x, sq, y, x3, q = (ph.sb(n, [P, C, T]) for n in ("o", "x", "sq", "y", "x3", "q"))
        hi, lo = ([ph.sb(f"{n}{i}", [P, C, T], F16) for i in range(2)] for n in ("hi", "lo"))
        mean, std = ph.sb("mean", [P, T]), ph.sb("std", [P, T])
        v = ph.sb("v", [P, C, E])
        psum = ph.ps("psum", [P, 8, T])
        loaded, product, drained, step = ph.sem("loaded"), ph.sem("product"), ph.sem("drained"), ph.sem("step")
        residual, centred, squared, normed, halves, stored = (
            ph.sem(n) for n in ("residual", "centred", "squared", "normed", "halves", "stored"))
        with nc.Block() as block:
            @block.sync
            def _(sp):
                load_weights(sp, loaded, [(W[n][:], chunked(w[n])) for n in W] + [(vec[n][:], w[n]) for n in vec]
                             + [(bv[:], w["v_b3"].unsqueeze(0))])

            @block.scalar
            def _(act):
                act.wait_ge(loaded, 16 * (len(W) + len(vec) + 1))
                nc.scalar.activation(vec["q_b3"][:], vec["q_b3"][:], ACT.Identity, scale=1.0 / 32).then_inc(step, 1)
        ph.renew()
        with nc.Fori(0, B) as b:
            with nc.Block() as block:
                @block.sync
                def _(sp):
                    sp.dma_start(o[:], rows_of(w["o2"], b)).then_inc(loaded, 16)
                    sp.dma_start(x[:], rows_of(w["x2"], b)).then_inc(loaded, 16)
                    sp.wait_ge(normed, C)
                    sp.dma_start(rows_of(w["x3"], b), x3[:]).then_inc(stored, 16)
                    sp.wait_ge(halves, 2)
                    split_store(sp, stored, w, "q3", b, E, hi[0], lo[0])
                    sp.wait_ge(halves, 4)
                    split_store(sp, stored, w, "kx", b, E, hi[1], lo[1])
                    sp.wait_ge(drained, 4 * C + 2)
                    for i in range(C):
                        dst = w["vx"].rearrange("(b g) s d -> b s g d", b=B)[b, i * P:(i + 1) * P]
                        sp.dma_start(dst, v[:, i, :].rearrange("p (g d) -> p g d", g=QUAD)).then_inc(stored, 16)
                    sp.wait_ge(stored, 16 * (5 + C))

                @block.tensor
                def _(pe):
                    group = Banks(nc, pe, psum, product, drained)

                    def project(weight, src):
                        for i in range(C):
                            group([(W[weight][:, c, i * P:(i + 1) * P], src[:, c, :]) for c in range(C)])

                    pe.wait_ge(loaded, 32)
                    project("Wo2", o)
                    pe.wait_ge(residual, 1)
                    norm_products(k, pe, group, x, sq, squared)
                    pe.wait_ge(normed, C)
                    project("q_w3", x3)
                    project("k_w3", x3)
                    for i in range(C):
                        group([(x3[:, c, i * P:(i + 1) * P], W["v_w3"][:, c, :]) for c in range(C)]
                              + [(k["ones"][0:1, :], bv[:])])

                @block.scalar
                def _(act):
                    drain = Drains(nc, act, psum, product, drained)
                    for c in range(C):
                        drain(y[:, c, :], ACT.Identity, bias=vec["bo2"][:, c:c + 1])
                    norm_drains(nc, act, drain, mean, y, sq, std, k["eps6"], centred, squared)
                    for c in range(C):
                        drain(q[:, c, :], ACT.Identity, scale=1.0 / 32, bias=vec["q_b3"][:, c:c + 1])
                    act.wait_ge(normed, C)
                    for c in range(C):
                        drain(y[:, c, :], ACT.Identity, bias=vec["k_b3"][:, c:c + 1])
                    for c in range(C):
                        drain(v[:, c, :], ACT.Identity)

                @block.vector
                def _(dve):
                    link = Chain(dve, step)
                    dve.wait_ge(loaded, 32)
                    dve.wait_ge(drained, C)
                    nc.vector.tensor_tensor(x[:], x[:], y[:], ALU.add).then_inc(residual, 1)
                    dve.wait_ge(residual, 1)
                    norm_steps(nc, dve, link, x, mean, y, std, vec["gamma2"], vec["beta2"], x3, drained, centred,
                               C + 1, C + 2, normed)
                    for n, (src, at) in enumerate(((q, 2 * C + 2), (y, 3 * C + 2))):
                        dve.wait_ge(drained, at)
                        nc.vector.tensor_copy(hi[n][:], src[:]).then_inc(halves, 1)
                        dve.wait_ge(halves, 2 * n + 1)
                        nc.vector.tensor_tensor(lo[n][:], src[:], hi[n][:], ALU.subtract).then_inc(halves, 1)
            ph.renew()


def final(nc, w, k, out):
    with ExitStack() as ctx:
        ph = Phase(nc, ctx, "mlp")
        F = 4 * E // P
        wo, w1, w2 = ph.sb("wo", [P, C, E]), ph.sb("w1", [P, C, 4 * E]), ph.sb("w2", [P, F, E])
        vec = {n: ph.sb(n, [P, m]) for n, m in (("out_b3", C), ("postnorm_w3", C), ("mlp_b13", F), ("mlp_b23", C))}
        o, x3, x, sq, y = (ph.sb(n, [P, C, T]) for n in ("o", "x3", "x", "sq", "y"))
        h = ph.sb("h", [P, F, T])
        std = ph.sb("std", [P, T])
        psum = ph.ps("psum", [P, 8, T])
        loaded, product, drained, step = ph.sem("loaded"), ph.sem("product"), ph.sem("drained"), ph.sem("step")
        residual, squared, normed, done, stored = (ph.sem(n) for n in ("residual", "squared", "normed", "done", "stored"))
        with nc.Block() as block:
            @block.sync
            def _(sp):
                load_weights(sp, loaded, [(wo[:], chunked(w["out_w3"])), (w1[:], chunked(w["mlp_w13"])),
                                          (w2[:], chunked(w["mlp_w23"]))] + [(vec[n][:], w[n]) for n in vec])
        ph.renew()
        with nc.Fori(0, B) as b:
            with nc.Block() as block:
                @block.sync
                def _(sp):
                    sp.dma_start(o[:], rows_of(w["o3"], b)).then_inc(loaded, 16)
                    sp.dma_start(x3[:], rows_of(w["x3"], b)).then_inc(loaded, 16)
                    sp.wait_ge(done, 1)
                    sp.dma_start(rows_of(out, b), x3[:]).then_inc(stored, 16)
                    sp.wait_ge(stored, 16)

                @block.tensor
                def _(pe):
                    group = Banks(nc, pe, psum, product, drained)
                    pe.wait_ge(loaded, 32)
                    for i in range(C):
                        group([(wo[:, c, i * P:(i + 1) * P], o[:, c, :]) for c in range(C)])
                    pe.wait_ge(squared, 1)
                    group([(k["mean"][:], sq[:, c, :]) for c in range(C)])
                    pe.wait_ge(normed, C)
                    for i in range(F):
                        group([(w1[:, c, i * P:(i + 1) * P], y[:, c, :]) for c in range(C)])
                    pe.wait_ge(drained, C + 1 + F)
                    for i in range(C):
                        group([(w2[:, f, i * P:(i + 1) * P], h[:, f, :]) for f in range(F)])

                @block.scalar
                def _(act):
                    drain = Drains(nc, act, psum, product, drained)
                    for c in range(C):
                        drain(y[:, c, :], ACT.Identity, bias=vec["out_b3"][:, c:c + 1])
                    act.wait_ge(residual, 1)
                    nc.scalar.activation(sq[:], x[:], ACT.Square).then_inc(squared, 1)
                    drain(std[:], ACT.Sqrt, bias=k["eps6"][:])
                    for f in range(F):
                        drain(h[:, f, :], ACT.Gelu_apprx_tanh, bias=vec["mlp_b13"][:, f:f + 1])
                    for c in range(C):
                        drain(sq[:, c, :], ACT.Identity, bias=vec["mlp_b23"][:, c:c + 1])

                @block.vector
                def _(dve):
                    link = Chain(dve, step)
                    dve.wait_ge(loaded, 32)
                    dve.wait_ge(drained, C)
                    nc.vector.tensor_tensor(x[:], x3[:], y[:], ALU.add).then_inc(residual, 1)
                    dve.wait_ge(residual, 1)
                    dve.wait_ge(drained, C + 1)
                    link(nc.vector.reciprocal(std[:], std[:]))
                    link(nc.vector.tensor_tensor(x[:], x[:], bc(std[:], C), ALU.mult))
                    for c in range(C):
                        nc.vector.tensor_scalar(y[:, c, :], x[:, c, :], vec["postnorm_w3"][:, c:c + 1], None,
                                                ALU.mult).then_inc(normed, 1)
                    dve.wait_ge(drained, 2 * C + 1 + F)
                    nc.vector.tensor_tensor(x3[:], x3[:], sq[:], ALU.add).then_inc(done, 1)
            ph.renew()


def build(nc, w, out):
    with ExitStack() as ctx:
        w = dict(w)
        scratch(nc, w)
        k = setup(nc, ctx, w)
        rwkv_inputs(nc, w, k)
        recurrence(nc, w, k)
        rwkv_outputs(nc, w, k)
        context_keys(nc, w, k)
        attention(nc, w, k, 1)
        between_1_2(nc, w, k)
        attention2(nc, w, k)
        between_2_3(nc, w, k)
        attention(nc, w, k, 3)
        final(nc, w, k, out)


def kernel(**inputs):
    import numpy as np
    import concourse.bacc as bacc
    from concourse import mybir as _mybir
    from concourse.bass_utils import run_bass_kernel_spmd

    nc = bacc.Bacc("TRN2", target_bir_lowering=False, num_devices=1)
    arrays = {f"in_{name}": a for name, a in layout(inputs).items()}
    w = {}
    for name, a in arrays.items():
        w[name[3:]] = nc.dram_tensor(name, a.shape, _mybir.dt.from_np(a.dtype), kind="ExternalInput").ap()
    out = nc.dram_tensor("out_t", (B, E, T), F32, kind="ExternalOutput").ap()
    build(nc, w, out)
    r = run_bass_kernel_spmd(nc, [arrays], core_ids=[0])
    return np.ascontiguousarray(np.transpose(r.results[0]["out_t"], (0, 2, 1)))


def layout(inputs):
    import numpy as np

    def tr(a):
        return np.ascontiguousarray(np.swapaxes(a, -1, -2))

    def col(v):
        return np.ascontiguousarray(v.reshape(-1, P).T)

    g = {n: np.asarray(a) for n, a in inputs.items()}
    L0 = {n[9:]: a for n, a in g.items() if n.startswith("L0_")}
    L1 = {n[9:]: a for n, a in g.items() if n.startswith("L1_")}
    L2 = {n[9:]: a for n, a in g.items() if n.startswith("L2_")}
    L3 = {n[9:]: a for n, a in g.items() if n.startswith("L3_")}
    ctx = g["ctx_2048"]
    o = {"x_t": tr(g["x"]), "ctx_t": tr(ctx)}
    for j in (0, 1):
        o[f"prev{j}"] = np.ascontiguousarray(ctx[:, j, :].reshape(B, C, P).transpose(0, 2, 1))
    o["state"] = np.ascontiguousarray(ctx[:, 2:2 + HS, :]).reshape(B, E, HS)
    for n in ("Wr", "Wk", "Wv", "Wg", "Wo"):
        o[n + "0"] = tr(L0[n])
    for n in ("ffn_Wk", "ffn_Wr", "ffn_Wv"):
        o[n] = tr(L0[n])
    o["maa_w2"] = np.ascontiguousarray(L0["maa_w2"]).reshape(160, E)
    o["faaaa"] = np.ascontiguousarray(L0["faaaa"]).reshape(E)
    for n in ("ln1_w", "ln1_b", "ln2_w", "ln2_b", "maa_x", "maa_w1", "maa_stack", "time_decay", "decay_w1",
              "decay_w2", "gn_w", "gn_b", "ffn_maa_k", "ffn_maa_r"):
        o[n] = np.ascontiguousarray(L0[n])
    for n in ("Wq", "Wk", "Wv", "Wo"):
        o[n + "1"] = tr(L1[n])
    for n in ("ln_gamma", "ln_beta", "gate"):
        o[n + "1"] = np.ascontiguousarray(L1[n])
    for n, a in L2.items():
        o[n + "2"] = np.ascontiguousarray(a)
    kv, kvb = L3.pop("kv_w"), L3.pop("kv_b")
    for j, n in enumerate("kv"):
        o[n + "_w3"] = np.ascontiguousarray(kv.reshape(E, E, 2)[..., j])
        o[n + "_b3"] = np.ascontiguousarray(kvb.reshape(E, 2)[..., j])
    for n, a in L3.items():
        o[n + "3"] = np.ascontiguousarray(a)
    o["mask1"] = np.ascontiguousarray(g["mask_BxS2_bf1"]).view(np.uint8)
    o["mask3"] = np.ascontiguousarray(g["mask_BxS2_ik0"])
    am = g["mask_Bx1xSxS2_ff0"][:, 0]
    o["mask2"] = np.ascontiguousarray(am)
    o["mask2_t"] = tr(am)
    i = np.arange(P)
    head, pos = i // HS, i % HS
    same = (head[:, None] == head[None, :])
    for n in ("ln1_w", "ln1_b", "ln2_w", "ln2_b", "maa_x", "time_decay", "gn_w", "gn_b", "ffn_maa_k", "ffn_maa_r", "faaaa",
              "ln_gamma1", "ln_beta1", "bq2", "bk2", "bo2", "gamma2", "beta2", "q_b3", "k_b3", "out_b3", "postnorm_w3",
              "mlp_b13", "mlp_b23"):
        o[n] = col(o[n])
    o["maa_stack"] = np.ascontiguousarray(o["maa_stack"].reshape(5, C, P).transpose(2, 0, 1))
    o["c_ident"] = np.eye(P, dtype=np.float32)
    o["c_head"] = same.astype(np.float32)
    d = np.arange(HS)
    o["c_sel"] = (same[:, None, :] & (pos[:, None, None] == d[None, :, None])).astype(np.float32)
    o["c_red"] = (same[:, None, :] & (pos[None, None, :] == d[None, :, None])).astype(np.float32)
    o["c_q"] = np.full((QUAD * T,), MASKED, np.float16)
    o["c_k"] = np.full((QUAD * (S2 + T),), -1.0, np.float16)
    o["c_ones"] = np.ones((P, 16, HS), np.float32)
    return o
```

```python
from contextlib import ExitStack

import concourse.bass as bass
from concourse import mybir

F32, F16 = mybir.dt.float32, mybir.dt.float16
U8, I32 = mybir.dt.uint8, mybir.dt.int32
ALU, ACT, AX = mybir.AluOpType, mybir.ActivationFunctionType, mybir.AxisListType

P = 128
B, T, E = 4, 512, 512
C = E // P
S2 = 1601
KT = 512
FULL, TAIL = S2 // KT, S2 % KT
HS = 16
MASKED = 32768.0
QUAD = 4


class Phase:

    def __init__(self, nc, ctx, tag):
        self.nc, self.ctx, self.tag, self.sems = nc, ctx, tag, []

    def sb(self, name, shape, dt=F32):
        return self.ctx.enter_context(self.nc.sbuf_tensor(f"{self.tag}_{name}", shape, dt))

    def ps(self, name, shape, dt=F32):
        return self.ctx.enter_context(self.nc.psum_tensor(f"{self.tag}_{name}", shape, dt))

    def sem(self, name):
        s = self.ctx.enter_context(self.nc.semaphore(f"{self.tag}_{name}"))
        self.sems.append(s)
        return s

    def renew(self):
        numbers = sorted(s.num for s in self.sems)
        if numbers[-1] - numbers[0] + 1 == len(numbers):
            self.nc.sync.sem_clear(range(numbers[0], numbers[-1] + 1))
        else:
            for s in self.sems:
                self.nc.sync.sem_clear(s)
        self.nc.all_engine_barrier()


class Chain:

    def __init__(self, eng, sem):
        self.eng, self.sem, self.n = eng, sem, 0

    def __call__(self, ins):
        ins.then_inc(self.sem, 1)
        self.n += 1
        self.eng.wait_ge(self.sem, self.n)


class Banks:

    def __init__(self, nc, pe, psum, product, drained):
        self.nc, self.pe, self.psum, self.product, self.drained, self.j = nc, pe, psum, product, drained, 0

    def __call__(self, pairs, m=P, n=T):
        if self.j >= 8:
            self.pe.wait_ge(self.drained, self.j - 7)
        out = self.psum[0:m, self.j % 8, 0:n]
        last = len(pairs) - 1
        for i, (lhsT, rhs) in enumerate(pairs):
            ins = self.nc.tensor.matmul(out, lhsT, rhs, start=i == 0, stop=i == last)
        ins.then_inc(self.product, 1)
        self.j += 1


class Drains:

    def __init__(self, nc, act, psum, product, drained):
        self.nc, self.act, self.psum, self.product, self.drained, self.j = nc, act, psum, product, drained, 0

    def __call__(self, out, func, m=P, n=T, **kw):
        self.act.wait_ge(self.product, self.j + 1)
        self.nc.scalar.activation(out, self.psum[0:m, self.j % 8, 0:n], func, **kw).then_inc(self.drained, 1)
        self.j += 1


def bc(ap, n):
    return ap.unsqueeze(1).broadcast_to([ap.shape[0], n, ap.shape[1]])


def load_weights(sp, sem, pairs):
    for dst, src in pairs:
        sp.dma_start(dst, src).then_inc(sem, 16)
    sp.wait_ge(sem, 16 * len(pairs))


def chunked(w):
    return w.rearrange("(c p) n -> p c n", p=P)


def column(v):
    return v


def setup(nc, ctx, w):
    ph = Phase(nc, ctx, "const")
    k = {}
    k["mean"] = ph.sb("mean", [P, P])
    k["ones"] = ph.sb("ones", [P, P])
    k["eps5"] = ph.sb("eps5", [P, 1])
    k["eps6"] = ph.sb("eps6", [P, 1])
    k["ident"] = ph.sb("ident", [P, P])
    k["sel"] = ph.sb("sel", [P, HS, P])
    k["red"] = ph.sb("red", [P, HS, P])
    k["head"] = ph.sb("head", [P, P])
    k["headmean"] = ph.sb("headmean", [P, P])
    loaded, made, step, stored = ph.sem("loaded"), ph.sem("made"), ph.sem("step"), ph.sem("stored")
    with ExitStack() as short:
        rows = Phase(nc, short, "masks")
        m8 = rows.sb("m8", [B, S2], U8)
        m32 = rows.sb("m32", [B, S2], I32)
        keep = rows.sb("keep", [B, S2])
        row1 = rows.sb("row1", [B, S2], F16)
        row3 = rows.sb("row3", [B, S2], F16)
        block = short.enter_context(nc.Block())

        @block.sync
        def _(sp):
            sp.dma_start(m8[:], w["mask1"]).then_inc(loaded, 16)
            sp.dma_start(m32[:], w["mask3"]).then_inc(loaded, 16)
            sp.dma_start(k["ident"][:], w["c_ident"]).then_inc(loaded, 16)
            sp.dma_start(k["sel"][:], w["c_sel"]).then_inc(loaded, 16)
            sp.dma_start(k["red"][:], w["c_red"]).then_inc(loaded, 16)
            sp.dma_start(k["head"][:], w["c_head"]).then_inc(loaded, 16)
            sp.wait_ge(made, 1)
            for name, row in (("km1", row1), ("km3", row3)):
                for g in range(w[name].shape[1]):
                    sp.dma_start(w[name][:, g, :], row[:]).then_inc(stored, 16)
            sp.wait_ge(stored, 16 * 2 * QUAD)

        @block.vector
        def _(dve):
            link = Chain(dve, step)
            link(nc.vector.memset(k["mean"][:], 1.0 / E))
            link(nc.vector.memset(k["ones"][:], 1.0))
            link(nc.vector.memset(k["eps5"][:], 1e-5))
            link(nc.vector.memset(k["eps6"][:], 1e-6))
            dve.wait_ge(loaded, 16 * 6)
            link(nc.vector.tensor_scalar(k["headmean"][:], k["head"][:], 1.0 / HS, None, ALU.mult))
            for m, row in ((m8, row1), (m32, row3)):
                link(nc.vector.tensor_copy(keep[:], m[:]))
                link(nc.vector.tensor_scalar(keep[:], keep[:], 0.0, MASKED, ALU.not_equal, ALU.mult))
                link(nc.vector.tensor_scalar(row[:], keep[:], MASKED, None, ALU.subtract))
            nc.vector.memset(m8[:], 0).then_inc(made, 1)
    ph.renew()
    return k


def rwkv_inputs(nc, w, k):
    with ExitStack() as ctx:
        ph = Phase(nc, ctx, "mix")
        W = {n: ph.sb(n, [P, C, E]) for n in ("Wr", "Wk", "Wv", "Wg")}
        w1 = ph.sb("w1", [P, C, 160])
        w2 = ph.sb("w2", [P, E])
        w2g = ph.sb("w2g", [32, E])
        dw1 = ph.sb("dw1", [P, C, 64])
        dw2 = ph.sb("dw2", [64, E])
        lnw, lnb, mx, td = (ph.sb(n, [P, C]) for n in ("lnw", "lnb", "mx", "td"))
        stack = ph.sb("stack", [P, 5, C])
        x, xc, sq = ph.sb("x", [P, C, T]), ph.sb("xc", [P, C, T]), ph.sb("sq", [P, C, T])
        xn = ph.sb("xn", [P, C, T + 1])
        prev = ph.sb("prev", [P, C])
        dx, u = ph.sb("dx", [P, C, T]), ph.sb("u", [P, C, T])
        mean, rstd = ph.sb("mean", [P, T]), ph.sb("rstd", [P, T])
        th, thg, dh_ = ph.sb("th", [P, T]), ph.sb("thg", [32, T]), ph.sb("dh", [64, T])
        mixed = [ph.sb(f"mixed{i}", [P, C, T]) for i in range(2)]
        y = [ph.sb(f"y{i}", [P, C, T]) for i in range(2)]
        psum = ph.ps("psum", [P, 8, T])
        loaded, product, drained, step = ph.sem("loaded"), ph.sem("product"), ph.sem("drained"), ph.sem("step")
        normed, squared, shifted, mixedup, ready = (ph.sem(n) for n in ("normed", "squared", "shifted", "mixedup", "ready"))
        centred, decays = ph.sem("centred"), ph.sem("decays")
        stored = [ph.sem(f"stored{i}") for i in range(2)]
        ORDER = (1, 0, 2, 3, 4)
        DEST = {0: "s_k", 1: "s_w", 2: "s_v", 3: "s_r", 4: "s_g"}
        WEIGHT = {0: "Wk", 2: "Wv", 3: "Wr", 4: "Wg"}

        with nc.Block() as block:
            @block.sync
            def _(sp):
                load_weights(sp, loaded, [(W[n][:], chunked(w[n + "0"])) for n in W] + [
                    (w1[:], chunked(w["maa_w1"])), (w2[:], w["maa_w2"][0:P, :]), (w2g[:], w["maa_w2"][P:P + 32, :]),
                    (dw1[:], chunked(w["decay_w1"])), (dw2[:], w["decay_w2"]), (lnw[:], column(w["ln1_w"])),
                    (lnb[:], column(w["ln1_b"])), (mx[:], column(w["maa_x"])), (td[:], column(w["time_decay"])),
                    (stack[:], w["maa_stack"])])
        ph.renew()

        first, at = {}, 4
        for n, i in enumerate(ORDER):
            if n == 0:
                first["mix", i] = at
                at += C
            if n + 1 < 5:
                first["mix", ORDER[n + 1]] = at
                at += C
            first["own", i] = at
            at += 1 + C if i == 1 else C

        with nc.Fori(0, B) as b:
            with nc.Block() as block:
                @block.sync
                def _(sp):
                    sp.dma_start(x[:], w["x_t"][b].rearrange("(c p) t -> p c t", p=P)).then_inc(loaded, 16)
                    sp.dma_start(prev[:], w["prev1"][b]).then_inc(loaded, 16)
                    for n, i in enumerate(ORDER):
                        sp.wait_ge(drained, first["own", i] + (1 + C if i == 1 else C))
                        if i == 1:
                            sp.wait_ge(decays, 1)
                        sp.dma_start(w[DEST[i]][b].rearrange("c p t -> p c t"), y[n % 2][:]).then_inc(stored[n % 2], 16)
                    sp.wait_ge(stored[0], 16 * 3)
                    sp.wait_ge(stored[1], 16 * 2)

                @block.tensor
                def _(pe):
                    group = Banks(nc, pe, psum, product, drained)
                    pe.wait_ge(loaded, 32)
                    group([(k["mean"][:], x[:, c, :]) for c in range(C)])
                    pe.wait_ge(squared, 1)
                    group([(k["mean"][:], sq[:, c, :]) for c in range(C)])
                    pe.wait_ge(shifted, 1)
                    group([(w1[:, c, 0:P], u[:, c, :]) for c in range(C)])
                    group([(w1[:, c, P:160], u[:, c, :]) for c in range(C)], m=32)

                    def mix(i):
                        for c in range(C):
                            f = slice(c * P, (c + 1) * P)
                            if i < 4:
                                r = slice(32 * i, 32 * i + 32)
                                group([(w2[r, f], th[r, :])])
                            else:
                                group([(w2g[:, f], thg[:])])

                    pe.wait_ge(drained, 4)
                    mix(ORDER[0])
                    for n, i in enumerate(ORDER):
                        if n + 1 < 5:
                            mix(ORDER[n + 1])
                        pe.wait_ge(mixedup, n + 1)
                        src = mixed[n % 2]
                        if i == 1:
                            group([(dw1[:, c, :], src[:, c, :]) for c in range(C)], m=64)
                            pe.wait_ge(drained, group.j)
                            for o in range(C):
                                group([(dw2[:, o * P:(o + 1) * P], dh_[:])])
                        else:
                            for o in range(C):
                                group([(W[WEIGHT[i]][:, c, o * P:(o + 1) * P], src[:, c, :]) for c in range(C)])

                @block.scalar
                def _(act):
                    drain = Drains(nc, act, psum, product, drained)
                    drain(mean[:], ACT.Identity)
                    act.wait_ge(centred, 1)
                    nc.scalar.activation(sq[:], xc[:], ACT.Square).then_inc(squared, 1)
                    drain(rstd[:], ACT.Sqrt, bias=k["eps5"][:])
                    drain(th[:], ACT.Tanh)
                    drain(thg[:], ACT.Tanh, m=32)

                    def mix(n, i):
                        dst = (sq, u)[n % 2]
                        if n >= 2:
                            act.wait_ge(mixedup, n - 1)
                        for c in range(C):
                            drain(dst[:, c, :], ACT.Identity, bias=stack[:, i, c:c + 1])

                    mix(0, ORDER[0])
                    for n, i in enumerate(ORDER):
                        if n + 1 < 5:
                            mix(n + 1, ORDER[n + 1])
                        if n >= 2:
                            act.wait_ge(stored[n % 2], 16 * (n // 2))
                        dst = y[n % 2]
                        if i == 1:
                            drain(dh_[:], ACT.Tanh, m=64)
                            for o in range(C):
                                drain(dst[:, o, :], ACT.Exp, bias=td[:, o:o + 1])
                            act.wait_ge(drained, drain.j)
                            nc.scalar.activation(dst[:], dst[:], ACT.Exp, scale=-1.0).then_inc(decays, 1)
                        else:
                            for o in range(C):
                                drain(dst[:, o, :], ACT.Silu if i == 4 else ACT.Identity)

                @block.vector
                def _(dve):
                    link = Chain(dve, step)
                    dve.wait_ge(loaded, 32)
                    link(nc.vector.tensor_copy(xn[:, :, 0], prev[:]))
                    dve.wait_ge(drained, 1)
                    nc.vector.tensor_tensor(xc[:], x[:], bc(mean[:], C), ALU.subtract).then_inc(centred, 1)
                    dve.wait_ge(centred, 1)
                    dve.wait_ge(drained, 2)
                    link(nc.vector.reciprocal(rstd[:], rstd[:]))
                    link(nc.vector.tensor_tensor(xc[:], xc[:], bc(rstd[:], C), ALU.mult))
                    for c in range(C):
                        link(nc.vector.tensor_scalar(xn[:, c, 1:], xc[:, c, :], lnw[:, c:c + 1], lnb[:, c:c + 1],
                                                     ALU.mult, ALU.add))
                    link(nc.vector.tensor_tensor(dx[:], xn[:, :, 0:T], xn[:, :, 1:], ALU.subtract))
                    for c in range(C):
                        ins = nc.vector.scalar_tensor_tensor(u[:, c, :], dx[:, c, :], mx[:, c:c + 1], xn[:, c, 1:],
                                                             ALU.mult, ALU.add)
                        link(ins) if c < C - 1 else ins.then_inc(shifted, 1)
                    for n, i in enumerate(ORDER):
                        dve.wait_ge(drained, first["mix", i] + C)
                        if n >= 2:
                            j = ORDER[n - 2]
                            dve.wait_ge(product, first["own", j] + (1 if j == 1 else C))
                        src, dst = (sq, u)[n % 2], mixed[n % 2]
                        link(nc.vector.tensor_tensor(dst[:], src[:], dx[:], ALU.mult))
                        nc.vector.tensor_tensor(dst[:], dst[:], xn[:, :, 1:], ALU.add).then_inc(mixedup, 1)
            ph.renew()


def recurrence(nc, w, k):
    with ExitStack() as ctx:
        ph = Phase(nc, ctx, "scan")
        src = {n: [ph.sb(f"{n}{i}", [P, T]) for i in range(2)] for n in "rkvw"}
        s0 = ph.sb("initial", [P, C, HS])
        bonus = ph.sb("bonus", [P, C])
        A = [ph.sb(f"a{i}", [P, T]) for i in range(2)]
        S = [ph.sb(f"states{i}", [P, T + 1]) for i in range(3)]
        Z = [ph.sb(f"z{i}", [P, T]) for i in range(3)]
        ruk = ph.sb("ruk", [P, T])
        bv = ph.sb("bv", [P, T])
        o = [ph.sb(f"o{i}", [P, T]) for i in range(2)]
        vb = ph.ps("vb", [P, 4, T])
        acc = ph.ps("acc", [P, 2, T])
        pb = ph.ps("pb", [P, T])
        loaded = [ph.sem(f"loaded{i}") for i in range(2)]
        first, spread, mul, scanned, zdone, reduced, rukdone, bonused, outdone, step, seeded = (
            ph.sem(n) for n in ("first", "spread", "mul", "scanned", "zdone", "reduced", "rukdone", "bonused", "outdone", "step", "seeded"))
        stored = [ph.sem(f"stored{i}") for i in range(2)]
        with nc.Block() as block:
            @block.sync
            def _(sp):
                load_weights(sp, first, [(bonus[:], column(w["faaaa"]))])
        ph.renew()
        LAG = 2
        with nc.Fori(0, B) as b:
            with nc.Block() as block:
                @block.sync
                def _(sp):
                    sp.dma_start(s0[:], w["state"][b].rearrange("(c p) d -> p c d", p=P)).then_inc(first, 16)

                    def load(c):
                        if c >= 2:
                            sp.wait_ge(outdone, c - 1)
                        for n in "rkvw":
                            sp.dma_start(src[n][c % 2][:], w["s_" + n][b, c]).then_inc(loaded[c % 2], 16)

                    load(0)
                    load(1)
                    for c in range(C):
                        sp.wait_ge(outdone, c + 1)
                        sp.dma_start(w["s_att"][b, c], o[c % 2][:]).then_inc(stored[c % 2], 16)
                        if c + 2 < C:
                            load(c + 2)
                    for half in stored:
                        sp.wait_ge(half, 16 * C // 2)

                @block.tensor
                def _(pe):
                    for c in range(C):
                        v = src["v"][c % 2]
                        pe.wait_ge(loaded[c % 2], 64 * (c // 2 + 1))
                        for d in range(HS + LAG):
                            if d < HS:
                                n = c * HS + d
                                if n >= 4:
                                    pe.wait_ge(mul, n - 3)
                                nc.tensor.matmul(vb[:, n % 4, :], k["sel"][:, d, :], v[:],
                                                 start=True, stop=True).then_inc(spread, 1)
                            if d == HS:
                                pe.wait_ge(rukdone, c + 1)
                                if c >= 1:
                                    pe.wait_ge(step, c)
                                nc.tensor.matmul(pb[:], k["head"][:], ruk[:], start=True, stop=True).then_inc(bonused, 1)
                            if d >= LAG:
                                m = c * HS + d - LAG
                                pe.wait_ge(zdone, m + 1)
                                if d == LAG and c >= 2:
                                    pe.wait_ge(outdone, c - 1)
                                nc.tensor.matmul(acc[:, c % 2, :], k["red"][:, d - LAG, :], Z[m % 3][:],
                                                 start=d == LAG, stop=d == HS + LAG - 1).then_inc(reduced, 1)

                @block.scalar
                def _(act):
                    act.wait_ge(first, 16)
                    for n in range(C * HS):
                        if n >= 3:
                            act.wait_ge(zdone, n - 2)
                            act.wait_ge(scanned, n - 2)
                        nc.scalar.activation(S[n % 3][:, 0:1], s0[:, n // HS, n % HS:n % HS + 1],
                                             ACT.Identity).then_inc(seeded, 1)

                @block.gpsimd
                def _(pool):
                    for n in range(C * HS):
                        pool.wait_ge(scanned, n + 1)
                        if n >= 3:
                            pool.wait_ge(reduced, n - 2)
                        nc.gpsimd.tensor_tensor(Z[n % 3][:], src["r"][n // HS % 2][:], S[n % 3][:, 0:T],
                                                ALU.mult).then_inc(zdone, 1)

                @block.vector
                def _(dve):
                    for c in range(C):
                        r, kk, v, dec = (src[n][c % 2] for n in "rkvw")
                        dve.wait_ge(loaded[c % 2], 64 * (c // 2 + 1))
                        for d in range(HS):
                            n = c * HS + d
                            dve.wait_ge(spread, n + 1)
                            if n >= 2:
                                dve.wait_ge(scanned, n - 1)
                            nc.vector.tensor_tensor(A[n % 2][:], kk[:], vb[:, n % 4, :], ALU.mult).then_inc(mul, 1)
                            dve.wait_ge(mul, n + 1)
                            dve.wait_ge(seeded, n + 1)
                            nc.vector.tensor_tensor_scan(S[n % 3][:, 1:], dec[:], A[n % 2][:], S[n % 3][:, 0:1],
                                                         ALU.mult, ALU.add).then_inc(scanned, 1)
                            if d == 1:
                                if c >= 1:
                                    dve.wait_ge(bonused, c)
                                nc.vector.scalar_tensor_tensor(ruk[:], r[:], bonus[:, c:c + 1], kk[:],
                                                               ALU.mult, ALU.mult).then_inc(rukdone, 1)
                        dve.wait_ge(bonused, c + 1)
                        nc.vector.tensor_tensor(bv[:], pb[:], v[:], ALU.mult).then_inc(step, 1)
                        dve.wait_ge(step, c + 1)
                        dve.wait_ge(reduced, HS * (c + 1))
                        if c >= 2:
                            dve.wait_ge(stored[c % 2], 16 * (c // 2))
                        nc.vector.tensor_tensor(o[c % 2][:], acc[:, c % 2, :], bv[:], ALU.add).then_inc(outdone, 1)
            ph.renew()


def rows_of(ap, b):
    if len(ap.shape) == 3:
        return ap[b].rearrange("(c p) t -> p c t", p=P)
    return ap.rearrange("(b c p) t -> b p c t", b=B, p=P)[b]


def norm_products(k, pe, group, x, squares, squared, n=T):
    group([(k["mean"][:], x[:, c, 0:n]) for c in range(C)], n=n)
    pe.wait_ge(squared, 1)
    group([(k["mean"][:], squares[:, c, 0:n]) for c in range(C)], n=n)


def norm_drains(nc, act, drain, mean, centred_x, squares, std, eps, centred, squared, n=T):
    drain(mean[:, 0:n], ACT.Identity, n=n)
    act.wait_ge(centred, 1)
    nc.scalar.activation(squares[:, :, 0:n], centred_x[:, :, 0:n], ACT.Square).then_inc(squared, 1)
    drain(std[:, 0:n], ACT.Sqrt, n=n, bias=eps[:])


def norm_steps(nc, dve, link, x, mean, centred_x, std, gamma, beta, out, drained, centred, mean_at, std_at, done, n=T):
    dve.wait_ge(drained, mean_at)
    nc.vector.tensor_tensor(centred_x[:, :, 0:n], x[:, :, 0:n], bc(mean[:, 0:n], C), ALU.subtract).then_inc(centred, 1)
    dve.wait_ge(centred, 1)
    dve.wait_ge(drained, std_at)
    link(nc.vector.reciprocal(std[:, 0:n], std[:, 0:n]))
    link(nc.vector.tensor_tensor(centred_x[:, :, 0:n], centred_x[:, :, 0:n], bc(std[:, 0:n], C), ALU.mult))
    for c in range(C):
        nc.vector.tensor_scalar(out[:, c, 0:n], centred_x[:, c, 0:n], gamma[:, c:c + 1], beta[:, c:c + 1],
                                ALU.mult, ALU.add).then_inc(done, 1)


def split_store(sp, sem, w, name, b, rows, hi, lo, cols=slice(0, T)):
    n = cols.stop - cols.start if isinstance(cols, slice) else T
    for part, half in (("hi", hi), ("lo", lo)):
        dst = w[name + part].rearrange("(b c p) t -> b p c t", b=B, p=P)[b]
        sp.dma_start(dst[:, :, cols], half[:, :, 0:n]).then_inc(sem, 16)


def rwkv_outputs(nc, w, k):
    with ExitStack() as ctx:
        ph = Phase(nc, ctx, "ffn")
        W = {n: ph.sb(n, [P, C, E]) for n in ("Wo0", "ffn_Wk", "ffn_Wr", "ffn_Wv", "Wq1")}
        vec = {n: ph.sb(n, [P, C]) for n in ("gn_w", "gn_b", "ln2_w", "ln2_b", "ffn_maa_k", "ffn_maa_r")}
        big = lambda n, dt=F32: ph.sb(n, [P, C, T], dt)
        att, gate, x, gmean, gstd, sq, o = (big(n) for n in ("att", "gate", "x", "gmean", "gstd", "sq", "o"))
        dx, kk, rr = big("dx"), big("kk"), big("rr")
        xn, prev = ph.sb("xn", [P, C, T + 1]), ph.sb("prev", [P, C])
        mean, std = ph.sb("mean", [P, T]), ph.sb("std", [P, T])
        qhi, qlo = big("qhi", F16), big("qlo", F16)
        psum = ph.ps("psum", [P, 8, T])
        loaded, product, drained, step = ph.sem("loaded"), ph.sem("product"), ph.sem("drained"), ph.sem("step")
        gcentred, gsquared, gated, residual, centred, squared, normed, mixed, relu2, done, halves, stored = (
            ph.sem(n) for n in ("gcentred", "gsquared", "gated", "residual", "centred", "squared", "normed", "mixed",
                                "relu2", "done", "halves", "stored"))
        with nc.Block() as block:
            @block.sync
            def _(sp):
                load_weights(sp, loaded, [(W[n][:], chunked(w[n])) for n in W] + [(vec[n][:], w[n]) for n in vec])
        ph.renew()
        with nc.Fori(0, B) as b:
            with nc.Block() as block:
                @block.sync
                def _(sp):
                    for dst, src in ((att, w["s_att"]), (gate, w["s_g"])):
                        sp.dma_start(dst[:], src[b].rearrange("c p t -> p c t")).then_inc(loaded, 16)
                    sp.dma_start(x[:], w["x_t"][b].rearrange("(c p) t -> p c t", p=P)).then_inc(loaded, 16)
                    sp.dma_start(prev[:], w["prev0"][b]).then_inc(loaded, 16)
                    sp.wait_ge(done, 1)
                    sp.dma_start(w["x1"][b].rearrange("(c p) t -> p c t", p=P), x[:]).then_inc(stored, 16)
                    sp.wait_ge(halves, 2)
                    split_store(sp, stored, w, "q1", b, E, qhi, qlo)
                    sp.wait_ge(stored, 48)

                @block.tensor
                def _(pe):
                    group = Banks(nc, pe, psum, product, drained)

                    def project(weight, src):
                        for o_ in range(C):
                            group([(W[weight][:, c, o_ * P:(o_ + 1) * P], src[:, c, 0:T]) for c in range(C)])

                    pe.wait_ge(loaded, 64)
                    for c in range(C):
                        group([(k["headmean"][:], att[:, c, :])])
                    pe.wait_ge(gsquared, 1)
                    for c in range(C):
                        group([(k["headmean"][:], sq[:, c, :])])
                    pe.wait_ge(gated, 1)
                    project("Wo0", att)
                    pe.wait_ge(residual, 1)
                    norm_products(k, pe, group, x, sq, squared)
                    pe.wait_ge(mixed, C)
                    project("ffn_Wk", gmean)
                    pe.wait_ge(mixed, 2 * C)
                    project("ffn_Wr", gstd)
                    pe.wait_ge(relu2, 1)
                    project("ffn_Wv", kk)
                    pe.wait_ge(done, 1)
                    project("Wq1", x)

                @block.scalar
                def _(act):
                    drain = Drains(nc, act, psum, product, drained)
                    for c in range(C):
                        drain(gmean[:, c, :], ACT.Identity)
                    act.wait_ge(gcentred, 1)
                    nc.scalar.activation(sq[:], att[:], ACT.Square).then_inc(gsquared, 1)
                    for c in range(C):
                        drain(gstd[:, c, :], ACT.Sqrt, bias=k["eps5"][:])
                    for c in range(C):
                        drain(o[:, c, :], ACT.Identity)
                    norm_drains(nc, act, drain, mean, o, sq, std, k["eps5"], centred, squared)
                    for c in range(C):
                        drain(kk[:, c, :], ACT.Relu)
                    for c in range(C):
                        drain(rr[:, c, :], ACT.Sigmoid)
                    for c in range(C):
                        drain(o[:, c, :], ACT.Identity)
                    for c in range(C):
                        drain(sq[:, c, :], ACT.Identity, scale=32 ** -0.5)

                @block.vector
                def _(dve):
                    link = Chain(dve, step)
                    dve.wait_ge(loaded, 64)
                    link(nc.vector.tensor_copy(xn[:, :, 0], prev[:]))
                    dve.wait_ge(drained, C)
                    nc.vector.tensor_tensor(att[:], att[:], gmean[:], ALU.subtract).then_inc(gcentred, 1)
                    dve.wait_ge(gcentred, 1)
                    dve.wait_ge(drained, 2 * C)
                    link(nc.vector.reciprocal(gstd[:], gstd[:]))
                    link(nc.vector.tensor_tensor(att[:], att[:], gstd[:], ALU.mult))
                    for c in range(C):
                        link(nc.vector.tensor_scalar(att[:, c, :], att[:, c, :], vec["gn_w"][:, c:c + 1],
                                                     vec["gn_b"][:, c:c + 1], ALU.mult, ALU.add))
                    nc.vector.tensor_tensor(att[:], att[:], gate[:], ALU.mult).then_inc(gated, 1)
                    dve.wait_ge(drained, 3 * C)
                    nc.vector.tensor_tensor(x[:], x[:], o[:], ALU.add).then_inc(residual, 1)
                    dve.wait_ge(residual, 1)
                    norm_steps(nc, dve, link, x, mean, o, std, vec["ln2_w"], vec["ln2_b"], xn[:, :, 1:], drained,
                               centred, 3 * C + 1, 3 * C + 2, normed)
                    dve.wait_ge(normed, C)
                    link(nc.vector.tensor_tensor(dx[:], xn[:, :, 0:T], xn[:, :, 1:], ALU.subtract))
                    for m, dst in (("ffn_maa_k", gmean), ("ffn_maa_r", gstd)):
                        for c in range(C):
                            nc.vector.scalar_tensor_tensor(dst[:, c, :], dx[:, c, :], vec[m][:, c:c + 1],
                                                           xn[:, c, 1:], ALU.mult, ALU.add).then_inc(mixed, 1)
                    dve.wait_ge(drained, 4 * C + 2)
                    nc.vector.tensor_tensor(kk[:], kk[:], kk[:], ALU.mult).then_inc(relu2, 1)
                    dve.wait_ge(drained, 6 * C + 2)
                    link(nc.vector.tensor_tensor(rr[:], rr[:], o[:], ALU.mult))
                    nc.vector.tensor_tensor(x[:], x[:], rr[:], ALU.add).then_inc(done, 1)
                    dve.wait_ge(drained, 7 * C + 2)
                    nc.vector.tensor_copy(qhi[:], sq[:]).then_inc(halves, 1)
                    dve.wait_ge(halves, 1)
                    nc.vector.tensor_tensor(qlo[:], sq[:], qhi[:], ALU.subtract).then_inc(halves, 1)
            ph.renew()


WSCALE = 32.0


class Halves:

    def __init__(self, hi, lo):
        self.hi, self.lo = hi, lo

    def __getitem__(self, at):
        return Halves(self.hi[at], self.lo[at])


def split_pairs(pairs):
    return [p for l, r in pairs for p in ((l.hi, r.hi), (l.hi, r.lo), (l.lo, r.hi))]


def split_weights(nc, ph, loaded, stages, parts):
    high, done = ph.splitting
    n = len(stages)
    for first in range(0, len(parts), n):
        round_ = parts[first:first + n]
        with nc.Block() as block:
            @block.sync
            def _(sp):
                load_weights(sp, loaded, [(stage, src) for stage, (_, src) in zip(stages, round_)])

            @block.vector
            def _(dve):
                dve.wait_ge(loaded, 16 * len(round_))
                for i, (stage, (dst, _)) in enumerate(zip(stages, round_)):
                    nc.vector.tensor_scalar(dst.hi, stage, WSCALE, None, ALU.mult).then_inc(high, 1)
                    dve.wait_ge(high, i + 1)
                    nc.vector.scalar_tensor_tensor(dst.lo, stage, WSCALE, dst.hi, ALU.mult, ALU.subtract).then_inc(done, 1)
                dve.wait_ge(done, len(round_))
        ph.renew()


def context_keys(nc, w, k):
    with ExitStack() as ctx:
        ph = Phase(nc, ctx, "ctx")
        W = {n: Halves(ph.sb(n + "h", [P, C, m], F16), ph.sb(n + "l", [P, C, m], F16))
             for n, m in (("Wk1", E), ("Wv1", E), ("k_w3", E), ("v_w3", E), ("Wk2", P), ("Wv2", P))}
        xs = [Halves(ph.sb(f"xh{i}", [P, C, KT], F16), ph.sb(f"xl{i}", [P, C, KT], F16)) for i in range(2)]
        as_ = Halves(ph.sb("ah", [P, C, KT], F16), ph.sb("al", [P, C, KT], F16))
        scaled_one = ph.sb("scaled_one", [1, P])
        vec = {"ln_gamma1": ph.sb("gamma", [P, C]), "ln_beta1": ph.sb("beta", [P, C]), "bk2": ph.sb("bk2", [P, 1]),
               "k_b3": ph.sb("bk3", [P, C])}
        row = {"bv2": ph.sb("bv2", [1, P]), "v_b3": ph.sb("bv3", [1, E])}
        x = [ph.sb(f"x{i}", [P, C, KT]) for i in range(2)]
        xc, sq, a = (ph.sb(n, [P, C, KT]) for n in ("xc", "sq", "a"))
        mean, std = ph.sb("mean", [P, KT]), ph.sb("std", [P, KT])
        kf = ph.sb("kf", [P, C, KT])
        hi, lo = ([ph.sb(f"{n}{i}", [P, C, KT], F16) for i in range(2)] for n in ("hi", "lo"))
        k2f, k2hi, k2lo = ph.sb("k2f", [P, 1, KT]), ph.sb("k2hi", [P, 1, KT], F16), ph.sb("k2lo", [P, 1, KT], F16)
        v = [ph.sb(f"v{i}", [P, E]) for i in range(4)]
        v2 = [ph.sb(f"v2{i}", [P, P]) for i in range(4)]
        psum = ph.ps("psum", [P, 8, KT])
        loaded, product, drained, step = ph.sem("loaded"), ph.sem("product"), ph.sem("drained"), ph.sem("step")
        centred, squared, normed, halves = (ph.sem(n) for n in ("centred", "squared", "normed", "halves"))
        ph.splitting = ph.sem("high"), ph.sem("low")
        xsplit, asplit = ph.sem("xsplit"), ph.sem("asplit")
        arrived = [ph.sem(f"arrived{i}") for i in range(2)]
        stored = {n: ph.sem(f"stored_{n}") for n in ("k1", "k2", "k3")}
        vstored = [ph.sem(f"vstored{i}") for i in range(4)]
        v2stored = [ph.sem(f"v2stored{i}") for i in range(4)]
        with nc.Block() as block:
            @block.sync
            def _(sp):
                load_weights(sp, loaded, [(vec[n][:], w[n]) for n in vec] + [(row[n][:], w[n].unsqueeze(0)) for n in row])

            @block.vector
            def _(dve):
                nc.vector.memset(scaled_one[:], WSCALE).then_inc(step, 1)
        ph.renew()
        split_weights(nc, ph, loaded, [t[:] for t in (x[0], x[1], xc, sq)],
                      [(W[n][:], chunked(w[n])) for n in ("Wk1", "Wv1", "k_w3", "v_w3")])
        split_weights(nc, ph, loaded, [t[:, :, 0:P] for t in (x[0], x[1])], [(W[n][:], chunked(w[n])) for n in ("Wk2", "Wv2")])

        class Tile:

            def __init__(self, i, base):
                self.i, self.base, self.t0 = i, base, i * KT
                self.n = n = min(KT, S2 - self.t0)
                self.width = [min(P, n - P * m) for m in range(-(-n // P))]
                tt = len(self.width)
                self.k2 = base + 2
                self.v2 = self.k2 + tt
                self.k3 = self.v2 + C
                self.v3 = self.k3 + tt
                self.std = self.v3 + 1
                self.k1 = self.std + C
                self.v1 = self.k1 + tt

        tiles = []
        for i in range(-(-S2 // KT)):
            tiles.append(Tile(i, tiles[-1].v1 if tiles else 0))

        with nc.Fori(0, B) as b:
            with nc.Block() as block:
                @block.sync
                def _(sp):
                    def load(t):
                        if t.i >= 2:
                            sp.wait_ge(product, tiles[t.i - 1].base)
                            sp.wait_ge(centred, t.i - 1)
                            sp.wait_ge(xsplit, 2 * (t.i - 1))
                        sp.dma_start(x[t.i % 2][:, :, 0:t.n],
                                     rows_of(w["ctx_t"], b)[:, :, t.t0:t.t0 + t.n]).then_inc(arrived[t.i % 2], 16)

                    def keys_out(t, count, name, hi_, lo_):
                        sp.wait_ge(halves, 6 * t.i + count)
                        for part, half in (("hi", hi_), ("lo", lo_)):
                            dst = rows_of(w[name + part], b)
                            sp.dma_start(dst[:, :, t.t0:t.t0 + t.n], half[:, :, 0:t.n]).then_inc(stored[name], 16)

                    def values_out(t, name, buf, end, sems):
                        for m, wd in enumerate(t.width):
                            sp.wait_ge(drained, end - len(t.width) + m + 1)
                            d = HS if name == "v2" else P
                            dst = w[name].rearrange("(b g) s d -> b s g d", b=B)[b, t.t0 + m * P:t.t0 + m * P + wd]
                            sp.dma_start(dst, buf[m][0:wd].rearrange("p (g d) -> p g d", d=d)).then_inc(sems[m], 16)

                    load(tiles[0])
                    load(tiles[1])
                    for t in tiles:
                        if 1 <= t.i < len(tiles) - 1:
                            load(tiles[t.i + 1])
                        values_out(t, "v2", v2, t.v2, v2stored)
                        keys_out(t, 2, "k2", k2hi, k2lo)
                        values_out(t, "v3", v, t.v3, vstored)
                        keys_out(t, 4, "k3", hi[0], lo[0])
                        values_out(t, "v1", v, t.v1, vstored)
                        keys_out(t, 6, "k1", hi[1], lo[1])
                    for n in stored:
                        sp.wait_ge(stored[n], 32 * len(tiles))
                    for m in range(4):
                        of = sum(1 for t in tiles if m < len(t.width))
                        sp.wait_ge(v2stored[m], 16 * of)
                        sp.wait_ge(vstored[m], 32 * of)

                @block.tensor
                def _(pe):
                    group = Banks(nc, pe, psum, product, drained)
                    for t in tiles:
                        n, xt = t.n, x[t.i % 2]

                        def keys(weight, src, chunks=C):
                            for o in range(chunks):
                                group(split_pairs([(W[weight][:, c, o * P:(o + 1) * P], src[:, c, 0:n])
                                                   for c in range(C)]), n=n)

                        def values(weight, src, bias=None, m=E):
                            for i, wd in enumerate(t.width):
                                pairs = split_pairs([(src[:, c, i * P:i * P + wd], W[weight][:, c, :]) for c in range(C)])
                                if bias is not None:
                                    pairs.append((scaled_one[0:1, 0:wd], bias[:]))
                                group(pairs, m=wd, n=m)

                        pe.wait_ge(arrived[t.i % 2], 16 * (t.i // 2 + 1))
                        group([(k["mean"][:], xt[:, c, 0:n]) for c in range(C)], n=n)
                        xh = xs[t.i % 2]
                        pe.wait_ge(xsplit, 2 * (t.i + 1))
                        keys("Wk2", xh, 1)
                        values("Wv2", xh, row["bv2"], P)
                        keys("k_w3", xh)
                        values("v_w3", xh, row["v_b3"])
                        pe.wait_ge(squared, t.i + 1)
                        group([(k["mean"][:], sq[:, c, 0:n]) for c in range(C)], n=n)
                        pe.wait_ge(asplit, 2 * (t.i + 1))
                        keys("Wk1", as_)
                        values("Wv1", as_)

                @block.scalar
                def _(act):
                    drain = Drains(nc, act, psum, product, drained)
                    for t in tiles:
                        n = t.n
                        if t.i:
                            act.wait_ge(centred, t.i)
                        drain(mean[:, 0:n], ACT.Identity, n=n)
                        if t.i:
                            act.wait_ge(halves, 6 * t.i - 4)
                        drain(k2f[:, 0, 0:n], ACT.Identity, n=n, scale=1.0 / WSCALE, bias=vec["bk2"][:])
                        for m, wd in enumerate(t.width):
                            if t.i:
                                act.wait_ge(v2stored[m], 16 * t.i)
                            drain(v2[m][0:wd], ACT.Identity, m=wd, n=P, scale=1.0 / WSCALE)
                        act.wait_ge(centred, t.i + 1)
                        if t.i:
                            act.wait_ge(product, tiles[t.i - 1].std)
                        nc.scalar.activation(sq[:, :, 0:n], xc[:, :, 0:n], ACT.Square).then_inc(squared, 1)
                        if t.i:
                            act.wait_ge(halves, 6 * t.i)
                        for o in range(C):
                            drain(kf[:, o, 0:n], ACT.Identity, n=n, scale=1.0 / WSCALE, bias=vec["k_b3"][:, o:o + 1])
                        for m, wd in enumerate(t.width):
                            if t.i:
                                act.wait_ge(vstored[m], 32 * t.i)
                            drain(v[m][0:wd], ACT.Identity, m=wd, n=E, scale=1.0 / WSCALE)
                        if t.i:
                            act.wait_ge(normed, C * t.i)
                        drain(std[:, 0:n], ACT.Sqrt, n=n, bias=k["eps5"][:])
                        act.wait_ge(halves, 6 * t.i + 4)
                        for o in range(C):
                            drain(kf[:, o, 0:n], ACT.Identity, n=n, scale=1.0 / WSCALE)
                        for m, wd in enumerate(t.width):
                            act.wait_ge(vstored[m], 32 * t.i + 16)
                            drain(v[m][0:wd], ACT.Identity, m=wd, n=E, scale=1.0 / WSCALE)

                @block.vector
                def _(dve):
                    link = Chain(dve, step)
                    for t in tiles:
                        n = t.n

                        def split(end, full, hi_, lo_, count, name):
                            dve.wait_ge(drained, end)
                            if t.i:
                                dve.wait_ge(stored[name], 32 * t.i)
                            nc.vector.tensor_copy(hi_[:, :, 0:n], full[:, :, 0:n]).then_inc(halves, 1)
                            dve.wait_ge(halves, 6 * t.i + count)
                            nc.vector.tensor_tensor(lo_[:, :, 0:n], full[:, :, 0:n], hi_[:, :, 0:n],
                                                    ALU.subtract).then_inc(halves, 1)

                        dve.wait_ge(arrived[t.i % 2], 16 * (t.i // 2 + 1))
                        xt, xh = x[t.i % 2], xs[t.i % 2]
                        if t.i >= 2:
                            dve.wait_ge(product, tiles[t.i - 2].v3)
                        nc.vector.tensor_copy(xh.hi[:, :, 0:n], xt[:, :, 0:n]).then_inc(xsplit, 1)
                        dve.wait_ge(xsplit, 2 * t.i + 1)
                        nc.vector.tensor_tensor(xh.lo[:, :, 0:n], xt[:, :, 0:n], xh.hi[:, :, 0:n], ALU.subtract).then_inc(xsplit, 1)
                        dve.wait_ge(drained, t.base + 1)
                        if t.i:
                            dve.wait_ge(normed, C * t.i)
                        nc.vector.tensor_tensor(xc[:, :, 0:n], x[t.i % 2][:, :, 0:n], bc(mean[:, 0:n], C),
                                                ALU.subtract).then_inc(centred, 1)
                        split(t.k2, k2f, k2hi, k2lo, 1, "k2")
                        split(t.k3, kf, hi[0], lo[0], 3, "k3")
                        dve.wait_ge(drained, t.std)
                        dve.wait_ge(centred, t.i + 1)
                        link(nc.vector.reciprocal(std[:, 0:n], std[:, 0:n]))
                        link(nc.vector.tensor_tensor(xc[:, :, 0:n], xc[:, :, 0:n], bc(std[:, 0:n], C), ALU.mult))
                        if t.i:
                            dve.wait_ge(asplit, 2 * t.i)
                        for c in range(C):
                            nc.vector.tensor_scalar(a[:, c, 0:n], xc[:, c, 0:n], vec["ln_gamma1"][:, c:c + 1],
                                                    vec["ln_beta1"][:, c:c + 1], ALU.mult, ALU.add).then_inc(normed, 1)
                        dve.wait_ge(normed, C * (t.i + 1))
                        if t.i:
                            dve.wait_ge(product, t.base)
                        nc.vector.tensor_copy(as_.hi[:, :, 0:n], a[:, :, 0:n]).then_inc(asplit, 1)
                        dve.wait_ge(asplit, 2 * t.i + 1)
                        nc.vector.tensor_tensor(as_.lo[:, :, 0:n], a[:, :, 0:n], as_.hi[:, :, 0:n], ALU.subtract).then_inc(asplit, 1)
                        split(t.k1, kf, hi[1], lo[1], 5, "k1")
            ph.renew()


def attention(nc, w, k, layer, add=False):
    dh = 16 if layer == 2 else 32
    latents = T if layer == 3 else 0
    NK = latents + S2
    NT = -(-NK // P)
    quads = E // dh // QUAD
    KH = 1 if layer == 2 else QUAD
    HALF = [("hi", "hi"), ("hi", "lo"), ("lo", "hi")] + ([("lo", "lo")] if dh == 16 else [])
    STACK = len(HALF) * dh
    WITH_ONES = layer == 2
    BANKS = 1 if WITH_ONES else 2
    RING1, RING2 = (4, 3) if WITH_ONES else (3, 3)
    MROW = P - 1
    PIECES = -(-NK // T)
    PIECE = -(-NK // PIECES)
    UNITS = QUAD * C * PIECES
    PER = -(-(UNITS + 1) // (NT - 2))
    END1 = UNITS // PER
    NB = 3
    OUTS = QUAD if dh < 32 else 1
    NP = 2 if WITH_ONES else 3
    PH = QUAD - 1
    PADDS, DADDS = PH * (NT - 1), NT - 1
    with ExitStack() as ctx:
        ph = Phase(nc, ctx, f"att{layer}{'m' if add else ''}")
        VC = 32 if WITH_ONES else P
        Q = [ph.sb(f"q{i}", [P, QUAD, T], F16) for i in range(NB)]
        K = [ph.sb(f"k{i}", [P, KH, NK], F16) for i in range(NB)]
        V = [ph.sb(f"v{i}", [P, NT, VC]) for i in range(NB)]
        prob = [ph.sb(f"prob{i}", [P, QUAD, T]) for i in range(NP)]
        acc = [ph.sb(f"acc{i}", [P, QUAD, T]) for i in range(0 if WITH_ONES else 2)]
        part = ph.sb("part", [P, QUAD * C, PIECES])
        top = ph.sb("top", [P, QUAD * C])
        topT = ph.sb("topT", [QUAD * C, P], F32 if add else F16)
        sums_sb = ph.sb("sums_sb", [P, T])
        recip, spread, out = ph.sb("recip", [P, T]), ph.sb("spread", [P, T]), ph.sb("out", [P, T])
        scores1 = ph.ps("scores1", [P, RING1, T])
        scores2 = ph.ps("scores2", [P, RING2, T])
        sums = ph.ps("sums", [P, BANKS, T])
        if add:
            mask = ph.sb("mask", [P, C, S2])
            mask_t = ph.sb("mask_t", [P, NT, T])
            junk = ph.sb("junk", [P, RING1, T], mybir.dt.bfloat16)
            summed = ph.sb("summed", [P, RING2, T])
            maxima = [ph.sb(f"maxima{i}", [P, QUAD, T]) for i in range(NB)]
        added, padded, dadded, denom = (ph.sem(n) for n in ("added", "padded", "dadded", "denom"))
        fixed, loaded = ph.sem("fixed"), [ph.sem(f"loaded{i}") for i in range(NB)]
        scored, reduced, maxed, turned, rounded, topout, topsent, cleared = (
            ph.sem(n) for n in ("scored", "reduced", "maxed", "turned", "rounded", "topout", "topsent", "cleared"))
        shifted, masked, exped, mixdone, evacuated, normed, stored, step = (
            ph.sem(n) for n in ("shifted", "masked", "exped", "mixdone", "evacuated", "normed", "stored", "step"))

        def once(b):
            with nc.Block() as block:
                @block.vector
                def _(dve):
                    for i in range(NB):
                        nc.vector.memset(Q[i][:], 0.0).then_inc(cleared, 1)
                        nc.vector.memset(K[i][:], 0.0).then_inc(cleared, 1)

                @block.sync
                def _(sp):
                    sp.wait_ge(cleared, 2 * NB)
                    moves = []
                    for i in range(NB):
                        moves.append((K[i][MROW:MROW + 1], w["c_k"][0:KH * NK].rearrange("(o h s) -> o h s", o=1, h=KH)))
                        moves.append((Q[i][STACK:STACK + 1], w["c_q"].rearrange("(o h s) -> o h s", o=1, h=QUAD)))
                        if WITH_ONES:
                            moves.append((V[i][:, :, HS:2 * HS], w["c_ones"][:, 0:NT]))
                    if add:
                        full = NT - 1
                        moves.append((mask[:], w["mask2"][b].rearrange("(c p) s -> p c s", p=P)))
                        moves.append((mask_t[:, 0:full], w["mask2_t"][b][0:full * P].rearrange("(c p) t -> p c t", p=P)))
                        moves.append((mask_t[0:NK - full * P, full], w["mask2_t"][b][full * P:NK]))
                    load_weights(sp, fixed, moves)
            ph.renew()

        LOADS = 2 * len(HALF) + 2 + (0 if layer == 2 else 1) + (4 if latents else 0)

        def load(sp, j, i):
            def go(dst, src):
                sp.dma_start(dst, src).then_inc(loaded[i], 16)

            rows = bass.ds(j * (QUAD * dh), QUAD * dh)
            krows = bass.ds(j * (KH * dh), KH * dh)
            for n, (qp, kp) in enumerate(HALF):
                r = slice(n * dh, (n + 1) * dh)
                go(Q[i][r], w[f"q{layer}{qp}"][rows].rearrange("(h d) t -> d h t", d=dh))
                go(K[i][r, :, latents:], w[f"k{layer}{kp}"][krows].rearrange("(h d) t -> d h t", d=dh))
                if latents:
                    go(K[i][r, :, 0:latents], w[f"kx{kp}"][krows].rearrange("(h d) t -> d h t", d=dh))
            lt, full = latents // P, S2 // P
            if latents:
                go(V[i][:, 0:lt], w["vx"][j].rearrange("(c p) d -> p c d", p=P))
            vc, v = HS if WITH_ONES else VC, w[f"v{layer}"]
            go(V[i][:, lt:lt + full, 0:vc], v[j, 0:full * P].rearrange("(c p) d -> p c d", p=P))
            go(V[i][0:S2 - full * P, lt + full, 0:vc], v[j, full * P:S2])
            if layer != 2:
                km = w[f"km{layer}"].rearrange("b g s -> (b g) s")[j]
                go(K[i][STACK:STACK + 1, :, latents:], km.unsqueeze(0).unsqueeze(0).broadcast_to([1, KH, S2]))

        def run(j, steps, left=None):
            left = left if left is not None else steps + 2
            plan = [(None, (j, 0), (j + 1, 1))] if steps == 0 else [
                ((j + s, s % NB), (j + s + 1, (s + 1) % NB) if s + 1 < left else None,
                 (j + s + 2, (s + 2) % NB) if s + 2 < left else None) for s in range(steps)]

            def loads(i, s):
                return sum(1 for _, _, ld in plan[:s] if ld and ld[1] == i) + (1 if steps == 0 and i == 0 else 0)

            n1 = sum(1 for _, p1, _ in plan if p1)
            with nc.Block() as block:
                @block.sync
                def _(sp):
                    seen1 = 0
                    if steps == 0:
                        load(sp, j, 0)
                    for s, (p2, p1, ld) in enumerate(plan):
                        if ld:
                            if s:
                                sp.wait_ge(mixdone, NT * s)
                            load(sp, *ld)
                        if s:
                            sp.wait_ge(normed, s)
                            rows = w[f"o{layer}"][bass.ds(plan[s - 1][0][0] * (QUAD * dh), QUAD * dh)]
                            for h in range(OUTS):
                                m = P if OUTS == 1 else dh
                                sp.dma_start(rows[h * m:(h + 1) * m], out[32 * h:32 * h + m]).then_inc(stored, 16)
                        if p1:
                            seen1 += 1
                            sp.wait_ge(rounded, seen1)
                            tops = w["tops_f32" if add else "tops"]
                            sp.dma_start(tops, topT[:]).then_inc(topout, 16)
                            sp.wait_ge(topout, 16 * seen1)
                            row = tops.rearrange("(o h c) t -> o h (c t)", o=1, h=QUAD)
                            sp.dma_start(maxima[p1[1]][:] if add else Q[p1[1]][MROW:MROW + 1],
                                         row.broadcast_to([P, QUAD, T]) if add else row).then_inc(topsent, 16)
                    if steps:
                        sp.wait_ge(normed, steps)
                        rows = w[f"o{layer}"][bass.ds(plan[-1][0][0] * (QUAD * dh), QUAD * dh)]
                        for h in range(OUTS):
                            m = P if OUTS == 1 else dh
                            sp.dma_start(rows[h * m:(h + 1) * m], out[32 * h:32 * h + m]).then_inc(stored, 16)
                        sp.wait_ge(stored, 16 * steps * OUTS)
                    if n1:
                        sp.wait_ge(topsent, 16 * n1)
                    for i in range(NB):
                        if loads(i, len(plan)):
                            sp.wait_ge(loaded[i], 16 * LOADS * loads(i, len(plan)))

                @block.tensor
                def _(pe):
                    seen1 = 0
                    for s, (p2, p1, _) in enumerate(plan):
                        def pass1():
                            i = p1[1]
                            if loads(i, s):
                                pe.wait_ge(loaded[i], 16 * LOADS * loads(i, s))
                            for u in range(UNITS + 1):
                                n = seen1 * (UNITS + 1) + u
                                if n >= RING1:
                                    pe.wait_ge(reduced, n - RING1 + 1)
                                if u == UNITS:
                                    pe.wait_ge(maxed, seen1 + 1)
                                    nc.tensor.transpose(scores1[0:QUAD * C, n % RING1, 0:P], top[:],
                                                        k["ident"][:]).then_inc(turned, 1)
                                else:
                                    h, c, piece = u // (C * PIECES), u // PIECES % C, u % PIECES
                                    k0, k1 = piece * PIECE, min(NK, (piece + 1) * PIECE)
                                    nc.tensor.matmul(scores1[:, n % RING1, 0:k1 - k0], Q[i][0:MROW, h, c * P:(c + 1) * P],
                                                     K[i][0:MROW, 0 if KH == 1 else h, k0:k1],
                                                     start=True, stop=True).then_inc(scored, 1)
                                yield

                        one = pass1() if p1 else iter(())
                        if p2:
                            i = p2[1]
                            used = MROW if add else MROW + 1
                            if s:
                                pe.wait_ge(topsent, 16 * s)

                            def shift(kt, h):
                                n = (s * NT + kt) * QUAD + h
                                kw = min(P, NK - kt * P)
                                if n >= RING2:
                                    pe.wait_ge(masked if add else exped, n - RING2 + 1)
                                nc.tensor.matmul(scores2[0:kw, n % RING2, :],
                                                 K[i][0:used, 0 if KH == 1 else h, kt * P:kt * P + kw],
                                                 Q[i][0:used, h, :], start=True, stop=True).then_inc(shifted, 1)

                            def mix(t):
                                kw = min(P, NK - t * P)
                                pe.wait_ge(exped, (s * NT + t + 1) * QUAD)
                                if t == 0 and s:
                                    pe.wait_ge(evacuated, s)
                                pr = prob[(s * NT + t) % NP]
                                for h in range(QUAD):
                                    v0 = 0 if KH == 1 else 32 * h
                                    ins = nc.tensor.matmul(sums[32 * h:32 * h + 32, 0, :], V[i][0:kw, t, v0:v0 + 32],
                                                           pr[0:kw, h, :], start=t == 0, stop=t == NT - 1,
                                                           tile_position=(0, 32 * h))
                                ins.then_inc(mixdone, 1)

                            def denominators(of):
                                pe.wait_ge(padded, (of + 1) * PADDS)
                                pe.wait_ge(dadded, (of + 1) * DADDS)
                                if of:
                                    pe.wait_ge(normed, of)
                                for h in range(QUAD):
                                    ins = nc.tensor.matmul(sums[32 * h:32 * h + 32, 1, :], k["ones"][:, 0:32],
                                                           acc[of % 2][:, h, :], start=True, stop=True,
                                                           tile_position=(0, 32 * h))
                                ins.then_inc(denom, 1)

                            for kt in range(NT + 1):
                                budget = PER if kt < NT else 0
                                for h in range(QUAD):
                                    if kt < NT:
                                        shift(kt, h)
                                    if budget:
                                        next(one, None)
                                        budget -= 1
                                if kt >= 1:
                                    mix(kt - 1)
                                if kt == 1 and s and BANKS == 2:
                                    denominators(s - 1)
                                for _ in range(budget):
                                    next(one, None)
                        for _ in one:
                            pass
                        if p2 and s == len(plan) - 1 and BANKS == 2:
                            denominators(s)
                        if p1:
                            seen1 += 1

                @block.scalar
                def _(act):
                    for s, (p2, p1, _) in enumerate(plan):
                        def top_row():
                            act.wait_ge(turned, s + 1)
                            if s:
                                act.wait_ge(topout, 16 * s)
                            slot = (s * (UNITS + 1) + UNITS) % RING1
                            nc.scalar.activation(topT[:], scores1[0:QUAD * C, slot, 0:P], ACT.Identity).then_inc(rounded, 1)

                        for kt in range(NT if p2 else 0):
                            g = s * NT + kt
                            if g >= NP:
                                act.wait_ge(mixdone, g - NP + 1)
                                if BANKS == 2:
                                    s_, kt_ = (g - NP) // NT, max(1, (g - NP) % NT)
                                    act.wait_ge(padded, s_ * PADDS + PH * kt_)
                                    act.wait_ge(dadded, s_ * DADDS + kt_)
                            kw = min(P, NK - kt * P)
                            for h in range(QUAD):
                                n = g * QUAD + h
                                act.wait_ge(masked if add else shifted, n + 1)
                                src = summed if add else scores2
                                nc.scalar.activation(prob[g % NP][0:kw, h, :], src[0:kw, n % RING2, :], ACT.Exp).then_inc(exped, 1)
                            if p1 and kt == END1:
                                top_row()
                        if not p2:
                            top_row()

                @block.gpsimd
                def _(pool):
                    for g in range(0 if BANKS == 1 else steps * NT):
                        s, kt = g // NT, g % NT
                        if kt == 0:
                            continue
                        kw = min(P, NK - kt * P)
                        if kt == 1 and s >= 2:
                            pool.wait_ge(denom, s - 1)
                        for h in range(PH):
                            n = s * PADDS + (kt - 1) * PH + h
                            pool.wait_ge(exped, g * QUAD + h + 1)
                            if kt > 1:
                                pool.wait_ge(padded, n - PH + 1)
                            so_far = prob[(g - 1) % NP] if kt == 1 else acc[s % 2]
                            nc.gpsimd.tensor_tensor(acc[s % 2][0:kw, h, :], so_far[0:kw, h, :], prob[g % NP][0:kw, h, :],
                                                    ALU.add).then_inc(padded, 1)

                @block.vector
                def _(dve):
                    link = Chain(dve, step)

                    def normalise(s):
                        if WITH_ONES:
                            swap = [(m + HS) % 32 for m in range(32)]
                            link(nc.vector.stream_shuffle(spread[:], sums_sb[:], swap))
                            yield
                        else:
                            dve.wait_ge(denom, s + 1)
                        for q in range(C):
                            cols = slice(q * P, (q + 1) * P)
                            link(nc.vector.reciprocal(recip[:, cols], spread[:, cols] if WITH_ONES else sums[:, 1, cols]))
                            yield
                        if s:
                            dve.wait_ge(stored, 16 * s * OUTS)
                        nc.vector.tensor_tensor(out[:], sums_sb[:], recip[:], ALU.mult).then_inc(normed, 1)

                    def add_up(s, kt):
                        g, kw, h = s * NT + kt, min(P, NK - kt * P), QUAD - 1
                        dve.wait_ge(exped, (g + 1) * QUAD)
                        if kt == 1 and s >= 2:
                            dve.wait_ge(denom, s - 1)
                        if kt > 1:
                            dve.wait_ge(dadded, s * DADDS + kt - 1)
                        so_far = prob[(g - 1) % NP] if kt == 1 else acc[s % 2]
                        nc.vector.tensor_tensor(acc[s % 2][0:kw, h, :], so_far[0:kw, h, :], prob[g % NP][0:kw, h, :],
                                                ALU.add).then_inc(dadded, 1)

                    pending = iter(())
                    for s, (p2, p1, _) in enumerate(plan):
                        def pass1():
                            for u in range(UNITS):
                                h, c, piece = u // (C * PIECES), u // PIECES % C, u % PIECES
                                n = s * (UNITS + 1) + u
                                k0, k1 = piece * PIECE, min(NK, (piece + 1) * PIECE)
                                dve.wait_ge(scored, s * UNITS + u + 1)
                                dst, src = part[:, h * C + c, piece:piece + 1], scores1[:, n % RING1, 0:k1 - k0]
                                if add:
                                    if n >= RING1:
                                        dve.wait_ge(reduced, n - RING1 + 1)
                                    nc.vector.tensor_tensor_reduce(
                                        out=junk[:, n % RING1, 0:k1 - k0], in0=src, in1=mask[:, c, k0:k1], scale=1.0,
                                        scalar=-3.0e38, op0=ALU.add, op1=ALU.max, accum_out=dst).then_inc(reduced, 1)
                                else:
                                    nc.vector.reduce_max(dst, src, AX.X).then_inc(reduced, 1)
                                if u % 3 == 2 and u > 2 * PER:
                                    next(pending, None)
                                if u % PER == 2 and u // PER >= 2 and p2 and BANKS == 2:
                                    add_up(s, u // PER - 1)
                                yield
                            dve.wait_ge(reduced, s * (UNITS + 1) + UNITS)
                            nc.vector.reduce_max(top[:], part[:], AX.X).then_inc(maxed, 1)
                            yield
                            dve.wait_ge(rounded, s + 1)
                            dve.wait_ge(maxed, s + 1)
                            nc.vector.memset(part[:], 0.0).then_inc(reduced, 1)
                            yield

                        one = pass1() if p1 else iter(())
                        if p2 and add:
                            units = UNITS + 1 if p1 else 0
                            if s:
                                dve.wait_ge(topsent, 16 * s)
                            for kt in range(NT):
                                kw = min(P, NK - kt * P)
                                budget = min(PER, units)
                                units -= budget
                                for h in range(QUAD):
                                    n = (s * NT + kt) * QUAD + h
                                    dve.wait_ge(shifted, n + 1)
                                    if n >= RING2:
                                        dve.wait_ge(exped, n - RING2 + 1)
                                    nc.vector.tensor_tensor(summed[0:kw, n % RING2, :], scores2[0:kw, n % RING2, :],
                                                            mask_t[0:kw, kt, :], ALU.add).then_inc(added, 1)
                                    dve.wait_ge(added, n + 1)
                                    nc.vector.tensor_tensor(summed[0:kw, n % RING2, :], summed[0:kw, n % RING2, :],
                                                            maxima[p2[1]][0:kw, h, :], ALU.subtract).then_inc(masked, 1)
                                    if budget:
                                        next(one, None)
                                        budget -= 1
                                for _ in range(budget):
                                    next(one, None)
                        for _ in one:
                            pass
                        for _ in pending:
                            pass
                        if p2:
                            if BANKS == 2:
                                for kt in range(max(1, (UNITS - 1 - 2) // PER if p1 else 1), NT):
                                    add_up(s, kt)
                            dve.wait_ge(mixdone, NT * (s + 1))
                            if s:
                                dve.wait_ge(normed, s)
                            nc.vector.tensor_copy(sums_sb[:], sums[:, 0, :]).then_inc(evacuated, 1)
                            dve.wait_ge(evacuated, s + 1)
                            pending = normalise(s)
                    for _ in pending:
                        pass
            ph.renew()

        def whole(first, count):
            turn = NB * (1 if add else 2)
            bodies = (count - 2) // turn
            run(first, 0)
            with nc.Fori(0, bodies) as i:
                run(first + i * turn, turn)
            rest = count - bodies * turn
            run(first + bodies * turn, rest, rest)

        if add:
            with nc.Fori(0, B) as b:
                once(b)
                whole(b * quads, quads)
        else:
            once(None)
            whole(0, B * quads)


def masks_at_all(nc, w, k):
    with ExitStack() as ctx:
        ph = Phase(nc, ctx, "anymask")
        m = [ph.sb(f"m{i}", [P, C, S2]) for i in range(2)]
        ends = ph.sb("ends", [P, 2 * B])
        odd, count = ph.sb("odd", [P, 2 * B]), ph.sb("count", [P, 2 * B])
        seen, flag = ph.sb("seen", [P, 1]), ph.sb("flag", [P, 1], I32)
        psum = ph.ps("psum", [P, T])
        loaded = [ph.sem(f"loaded{i}") for i in range(2)]
        reduced, marked, summed, made, step, stored = (
            ph.sem(n) for n in ("reduced", "marked", "summed", "made", "step", "stored"))
        with nc.Block() as block:
            @block.sync
            def _(sp):
                for b in range(B):
                    if b >= 2:
                        sp.wait_ge(reduced, 2 * (b - 1))
                    sp.dma_start(m[b % 2][:], w["mask2"][b].rearrange("(c p) s -> p c s", p=P)).then_inc(loaded[b % 2], 16)
                sp.wait_ge(made, 1)
                sp.dma_start(w["anymask"], flag[0:1, :]).then_inc(stored, 16)
                sp.wait_ge(stored, 16)

            @block.tensor
            def _(pe):
                pe.wait_ge(marked, 1)
                nc.tensor.matmul(psum[:, 0:2 * B], k["ones"][:], odd[:], start=True, stop=True).then_inc(summed, 1)

            @block.vector
            def _(dve):
                link = Chain(dve, step)
                for b in range(B):
                    dve.wait_ge(loaded[b % 2], 16 * (b // 2 + 1))
                    flat = m[b % 2][:].rearrange("p c s -> p (c s)")
                    nc.vector.reduce_max(ends[:, 2 * b:2 * b + 1], flat, AX.X).then_inc(reduced, 1)
                    nc.vector.tensor_reduce(ends[:, 2 * b + 1:2 * b + 2], flat, AX.X, ALU.min).then_inc(reduced, 1)
                dve.wait_ge(reduced, 2 * B)
                nc.vector.tensor_scalar(odd[:], ends[:], 0.0, None, ALU.not_equal).then_inc(marked, 1)
                dve.wait_ge(summed, 1)
                link(nc.vector.tensor_copy(count[:], psum[:, 0:2 * B]))
                link(nc.vector.reduce_max(seen[:], count[:], AX.X))
                link(nc.vector.tensor_scalar(seen[:], seen[:], 0.0, None, ALU.not_equal))
                nc.vector.tensor_copy(flag[:], seen[:]).then_inc(made, 1)
        ph.renew()
    return nc.values_load(w["anymask"], min_val=0, max_val=1)


def attention2(nc, w, k):
    some = masks_at_all(nc, w, k)
    with nc.If(some == 0):
        attention(nc, w, k, 2)
    with nc.Else():
        attention(nc, w, k, 2, add=True)


def scratch(nc, w):
    def dram(name, shape, dt=F32):
        w[name] = nc.dram_tensor(name, shape, dt).ap()

    for n in "rkvwg":
        dram("s_" + n, [B, C, P, T])
    dram("s_att", [B, C, P, T])
    for n in ("km1", "km3"):
        dram(n, [B, QUAD, S2], F16)
    for n in ("x1", "x2", "x3"):
        dram(n, [B, E, T])
    for n in ("o1", "o2", "o3"):
        dram(n, [B * E, T])
    for j in (1, 2, 3):
        for part in ("hi", "lo"):
            dram(f"q{j}{part}", [B * E, T], F16)
    for j, rows in ((1, E), (2, P), (3, E)):
        for part in ("hi", "lo"):
            dram(f"k{j}{part}", [B * rows, S2], F16)
    for part in ("hi", "lo"):
        dram(f"kx{part}", [B * E, T], F16)
    dram("v1", [B * QUAD, S2, P])
    dram("v2", [B * 8, S2, HS])
    dram("v3", [B * QUAD, S2, P])
    dram("vx", [B * QUAD, T, P])
    dram("tops", [QUAD * C, P], F16)
    dram("anymask", [1, 1], I32)
    dram("tops_f32", [QUAD * C, P])


def between_1_2(nc, w, k):
    with ExitStack() as ctx:
        ph = Phase(nc, ctx, "mid1")
        W = {n: ph.sb(n, [P, C, E]) for n in ("Wo1", "Wq2")}
        bq, gate = ph.sb("bq", [P, C]), ph.sb("gate", [P, 1])
        o, x, y, q = (ph.sb(n, [P, C, T]) for n in ("o", "x", "y", "q"))
        qhi, qlo = ph.sb("qhi", [P, C, T], F16), ph.sb("qlo", [P, C, T], F16)
        psum = ph.ps("psum", [P, 8, T])
        loaded, product, drained, step = ph.sem("loaded"), ph.sem("product"), ph.sem("drained"), ph.sem("step")
        done, halves, stored = ph.sem("done"), ph.sem("halves"), ph.sem("stored")
        with nc.Block() as block:
            @block.sync
            def _(sp):
                load_weights(sp, loaded, [(W[n][:], chunked(w[n])) for n in W] + [
                    (bq[:], w["bq2"]), (gate[:], w["gate1"].unsqueeze(0).broadcast_to([P, 1]))])

            @block.scalar
            def _(act):
                act.wait_ge(loaded, 64)
                nc.scalar.activation(gate[:], gate[:], ACT.Tanh).then_inc(step, 1)
                nc.scalar.activation(bq[:], bq[:], ACT.Identity, scale=HS ** -0.5).then_inc(step, 1)
        ph.renew()
        with nc.Fori(0, B) as b:
            with nc.Block() as block:
                @block.sync
                def _(sp):
                    sp.dma_start(o[:], rows_of(w["o1"], b)).then_inc(loaded, 16)
                    sp.dma_start(x[:], rows_of(w["x1"], b)).then_inc(loaded, 16)
                    sp.wait_ge(done, 1)
                    sp.dma_start(rows_of(w["x2"], b), x[:]).then_inc(stored, 16)
                    sp.wait_ge(halves, 2)
                    split_store(sp, stored, w, "q2", b, E, qhi, qlo)
                    sp.wait_ge(stored, 48)

                @block.tensor
                def _(pe):
                    group = Banks(nc, pe, psum, product, drained)
                    pe.wait_ge(loaded, 32)
                    for i in range(C):
                        group([(W["Wo1"][:, c, i * P:(i + 1) * P], o[:, c, :]) for c in range(C)])
                    pe.wait_ge(done, 1)
                    for i in range(C):
                        group([(W["Wq2"][:, c, i * P:(i + 1) * P], x[:, c, :]) for c in range(C)])

                @block.scalar
                def _(act):
                    drain = Drains(nc, act, psum, product, drained)
                    for c in range(C):
                        drain(y[:, c, :], ACT.Identity, scale=gate[:])
                    for c in range(C):
                        drain(q[:, c, :], ACT.Identity, scale=HS ** -0.5, bias=bq[:, c:c + 1])

                @block.vector
                def _(dve):
                    dve.wait_ge(loaded, 32)
                    dve.wait_ge(drained, C)
                    nc.vector.tensor_tensor(x[:], x[:], y[:], ALU.add).then_inc(done, 1)
                    dve.wait_ge(drained, 2 * C)
                    nc.vector.tensor_copy(qhi[:], q[:]).then_inc(halves, 1)
                    dve.wait_ge(halves, 1)
                    nc.vector.tensor_tensor(qlo[:], q[:], qhi[:], ALU.subtract).then_inc(halves, 1)
            ph.renew()


def between_2_3(nc, w, k):
    with ExitStack() as ctx:
        ph = Phase(nc, ctx, "mid2")
        W = {n: ph.sb(n, [P, C, E]) for n in ("Wo2", "q_w3", "k_w3", "v_w3")}
        vec = {n: ph.sb(n, [P, C]) for n in ("bo2", "gamma2", "beta2", "q_b3", "k_b3")}
        bv = ph.sb("bv", [1, E])
        o, x, sq, y, x3, q = (ph.sb(n, [P, C, T]) for n in ("o", "x", "sq", "y", "x3", "q"))
        hi, lo = ([ph.sb(f"{n}{i}", [P, C, T], F16) for i in range(2)] for n in ("hi", "lo"))
        mean, std = ph.sb("mean", [P, T]), ph.sb("std", [P, T])
        v = ph.sb("v", [P, C, E])
        psum = ph.ps("psum", [P, 8, T])
        loaded, product, drained, step = ph.sem("loaded"), ph.sem("product"), ph.sem("drained"), ph.sem("step")
        residual, centred, squared, normed, halves, stored = (
            ph.sem(n) for n in ("residual", "centred", "squared", "normed", "halves", "stored"))
        with nc.Block() as block:
            @block.sync
            def _(sp):
                load_weights(sp, loaded, [(W[n][:], chunked(w[n])) for n in W] + [(vec[n][:], w[n]) for n in vec]
                             + [(bv[:], w["v_b3"].unsqueeze(0))])

            @block.scalar
            def _(act):
                act.wait_ge(loaded, 16 * (len(W) + len(vec) + 1))
                nc.scalar.activation(vec["q_b3"][:], vec["q_b3"][:], ACT.Identity, scale=1.0 / 32).then_inc(step, 1)
        ph.renew()
        with nc.Fori(0, B) as b:
            with nc.Block() as block:
                @block.sync
                def _(sp):
                    sp.dma_start(o[:], rows_of(w["o2"], b)).then_inc(loaded, 16)
                    sp.dma_start(x[:], rows_of(w["x2"], b)).then_inc(loaded, 16)
                    sp.wait_ge(normed, C)
                    sp.dma_start(rows_of(w["x3"], b), x3[:]).then_inc(stored, 16)
                    sp.wait_ge(halves, 2)
                    split_store(sp, stored, w, "q3", b, E, hi[0], lo[0])
                    sp.wait_ge(halves, 4)
                    split_store(sp, stored, w, "kx", b, E, hi[1], lo[1])
                    sp.wait_ge(drained, 4 * C + 2)
                    for i in range(C):
                        dst = w["vx"].rearrange("(b g) s d -> b s g d", b=B)[b, i * P:(i + 1) * P]
                        sp.dma_start(dst, v[:, i, :].rearrange("p (g d) -> p g d", g=QUAD)).then_inc(stored, 16)
                    sp.wait_ge(stored, 16 * (5 + C))

                @block.tensor
                def _(pe):
                    group = Banks(nc, pe, psum, product, drained)

                    def project(weight, src):
                        for i in range(C):
                            group([(W[weight][:, c, i * P:(i + 1) * P], src[:, c, :]) for c in range(C)])

                    pe.wait_ge(loaded, 32)
                    project("Wo2", o)
                    pe.wait_ge(residual, 1)
                    norm_products(k, pe, group, x, sq, squared)
                    pe.wait_ge(normed, C)
                    project("q_w3", x3)
                    project("k_w3", x3)
                    for i in range(C):
                        group([(x3[:, c, i * P:(i + 1) * P], W["v_w3"][:, c, :]) for c in range(C)]
                              + [(k["ones"][0:1, :], bv[:])])

                @block.scalar
                def _(act):
                    drain = Drains(nc, act, psum, product, drained)
                    for c in range(C):
                        drain(y[:, c, :], ACT.Identity, bias=vec["bo2"][:, c:c + 1])
                    norm_drains(nc, act, drain, mean, y, sq, std, k["eps6"], centred, squared)
                    for c in range(C):
                        drain(q[:, c, :], ACT.Identity, scale=1.0 / 32, bias=vec["q_b3"][:, c:c + 1])
                    act.wait_ge(normed, C)
                    for c in range(C):
                        drain(y[:, c, :], ACT.Identity, bias=vec["k_b3"][:, c:c + 1])
                    for c in range(C):
                        drain(v[:, c, :], ACT.Identity)

                @block.vector
                def _(dve):
                    link = Chain(dve, step)
                    dve.wait_ge(loaded, 32)
                    dve.wait_ge(drained, C)
                    nc.vector.tensor_tensor(x[:], x[:], y[:], ALU.add).then_inc(residual, 1)
                    dve.wait_ge(residual, 1)
                    norm_steps(nc, dve, link, x, mean, y, std, vec["gamma2"], vec["beta2"], x3, drained, centred,
                               C + 1, C + 2, normed)
                    for n, (src, at) in enumerate(((q, 2 * C + 2), (y, 3 * C + 2))):
                        dve.wait_ge(drained, at)
                        nc.vector.tensor_copy(hi[n][:], src[:]).then_inc(halves, 1)
                        dve.wait_ge(halves, 2 * n + 1)
                        nc.vector.tensor_tensor(lo[n][:], src[:], hi[n][:], ALU.subtract).then_inc(halves, 1)
            ph.renew()


def final(nc, w, k, out):
    with ExitStack() as ctx:
        ph = Phase(nc, ctx, "mlp")
        F = 4 * E // P
        wo, w1, w2 = ph.sb("wo", [P, C, E]), ph.sb("w1", [P, C, 4 * E]), ph.sb("w2", [P, F, E])
        vec = {n: ph.sb(n, [P, m]) for n, m in (("out_b3", C), ("postnorm_w3", C), ("mlp_b13", F), ("mlp_b23", C))}
        o, x3, x, sq, y = (ph.sb(n, [P, C, T]) for n in ("o", "x3", "x", "sq", "y"))
        h = ph.sb("h", [P, F, T])
        std = ph.sb("std", [P, T])
        psum = ph.ps("psum", [P, 8, T])
        loaded, product, drained, step = ph.sem("loaded"), ph.sem("product"), ph.sem("drained"), ph.sem("step")
        residual, squared, normed, done, stored = (ph.sem(n) for n in ("residual", "squared", "normed", "done", "stored"))
        with nc.Block() as block:
            @block.sync
            def _(sp):
                load_weights(sp, loaded, [(wo[:], chunked(w["out_w3"])), (w1[:], chunked(w["mlp_w13"])),
                                          (w2[:], chunked(w["mlp_w23"]))] + [(vec[n][:], w[n]) for n in vec])
        ph.renew()
        with nc.Fori(0, B) as b:
            with nc.Block() as block:
                @block.sync
                def _(sp):
                    sp.dma_start(o[:], rows_of(w["o3"], b)).then_inc(loaded, 16)
                    sp.dma_start(x3[:], rows_of(w["x3"], b)).then_inc(loaded, 16)
                    sp.wait_ge(done, 1)
                    sp.dma_start(rows_of(out, b), x3[:]).then_inc(stored, 16)
                    sp.wait_ge(stored, 16)

                @block.tensor
                def _(pe):
                    group = Banks(nc, pe, psum, product, drained)
                    pe.wait_ge(loaded, 32)
                    for i in range(C):
                        group([(wo[:, c, i * P:(i + 1) * P], o[:, c, :]) for c in range(C)])
                    pe.wait_ge(squared, 1)
                    group([(k["mean"][:], sq[:, c, :]) for c in range(C)])
                    pe.wait_ge(normed, C)
                    for i in range(F):
                        group([(w1[:, c, i * P:(i + 1) * P], y[:, c, :]) for c in range(C)])
                    pe.wait_ge(drained, C + 1 + F)
                    for i in range(C):
                        group([(w2[:, f, i * P:(i + 1) * P], h[:, f, :]) for f in range(F)])

                @block.scalar
                def _(act):
                    drain = Drains(nc, act, psum, product, drained)
                    for c in range(C):
                        drain(y[:, c, :], ACT.Identity, bias=vec["out_b3"][:, c:c + 1])
                    act.wait_ge(residual, 1)
                    nc.scalar.activation(sq[:], x[:], ACT.Square).then_inc(squared, 1)
                    drain(std[:], ACT.Sqrt, bias=k["eps6"][:])
                    for f in range(F):
                        drain(h[:, f, :], ACT.Gelu_apprx_tanh, bias=vec["mlp_b13"][:, f:f + 1])
                    for c in range(C):
                        drain(sq[:, c, :], ACT.Identity, bias=vec["mlp_b23"][:, c:c + 1])

                @block.vector
                def _(dve):
                    link = Chain(dve, step)
                    dve.wait_ge(loaded, 32)
                    dve.wait_ge(drained, C)
                    nc.vector.tensor_tensor(x[:], x3[:], y[:], ALU.add).then_inc(residual, 1)
                    dve.wait_ge(residual, 1)
                    dve.wait_ge(drained, C + 1)
                    link(nc.vector.reciprocal(std[:], std[:]))
                    link(nc.vector.tensor_tensor(x[:], x[:], bc(std[:], C), ALU.mult))
                    for c in range(C):
                        nc.vector.tensor_scalar(y[:, c, :], x[:, c, :], vec["postnorm_w3"][:, c:c + 1], None,
                                                ALU.mult).then_inc(normed, 1)
                    dve.wait_ge(drained, 2 * C + 1 + F)
                    nc.vector.tensor_tensor(x3[:], x3[:], sq[:], ALU.add).then_inc(done, 1)
            ph.renew()


def build(nc, w, out):
    with ExitStack() as ctx:
        w = dict(w)
        scratch(nc, w)
        k = setup(nc, ctx, w)
        rwkv_inputs(nc, w, k)
        recurrence(nc, w, k)
        rwkv_outputs(nc, w, k)
        context_keys(nc, w, k)
        attention(nc, w, k, 1)
        between_1_2(nc, w, k)
        attention2(nc, w, k)
        between_2_3(nc, w, k)
        attention(nc, w, k, 3)
        final(nc, w, k, out)


def kernel(**inputs):
    import numpy as np
    import concourse.bacc as bacc
    from concourse import mybir as _mybir
    from concourse.bass_utils import run_bass_kernel_spmd

    nc = bacc.Bacc("TRN2", target_bir_lowering=False, num_devices=1)
    arrays = {f"in_{name}": a for name, a in layout(inputs).items()}
    w = {}
    for name, a in arrays.items():
        w[name[3:]] = nc.dram_tensor(name, a.shape, _mybir.dt.from_np(a.dtype), kind="ExternalInput").ap()
    out = nc.dram_tensor("out_t", (B, E, T), F32, kind="ExternalOutput").ap()
    build(nc, w, out)
    r = run_bass_kernel_spmd(nc, [arrays], core_ids=[0])
    return np.ascontiguousarray(np.transpose(r.results[0]["out_t"], (0, 2, 1)))


def layout(inputs):
    import numpy as np

    def tr(a):
        return np.ascontiguousarray(np.swapaxes(a, -1, -2))

    def col(v):
        return np.ascontiguousarray(v.reshape(-1, P).T)

    g = {n: np.asarray(a) for n, a in inputs.items()}
    L0 = {n[9:]: a for n, a in g.items() if n.startswith("L0_")}
    L1 = {n[9:]: a for n, a in g.items() if n.startswith("L1_")}
    L2 = {n[9:]: a for n, a in g.items() if n.startswith("L2_")}
    L3 = {n[9:]: a for n, a in g.items() if n.startswith("L3_")}
    ctx = g["ctx_2048"]
    o = {"x_t": tr(g["x"]), "ctx_t": tr(ctx)}
    for j in (0, 1):
        o[f"prev{j}"] = np.ascontiguousarray(ctx[:, j, :].reshape(B, C, P).transpose(0, 2, 1))
    o["state"] = np.ascontiguousarray(ctx[:, 2:2 + HS, :]).reshape(B, E, HS)
    for n in ("Wr", "Wk", "Wv", "Wg", "Wo"):
        o[n + "0"] = tr(L0[n])
    for n in ("ffn_Wk", "ffn_Wr", "ffn_Wv"):
        o[n] = tr(L0[n])
    o["maa_w2"] = np.ascontiguousarray(L0["maa_w2"]).reshape(160, E)
    o["faaaa"] = np.ascontiguousarray(L0["faaaa"]).reshape(E)
    for n in ("ln1_w", "ln1_b", "ln2_w", "ln2_b", "maa_x", "maa_w1", "maa_stack", "time_decay", "decay_w1",
              "decay_w2", "gn_w", "gn_b", "ffn_maa_k", "ffn_maa_r"):
        o[n] = np.ascontiguousarray(L0[n])
    for n in ("Wq", "Wk", "Wv", "Wo"):
        o[n + "1"] = tr(L1[n])
    for n in ("ln_gamma", "ln_beta", "gate"):
        o[n + "1"] = np.ascontiguousarray(L1[n])
    for n, a in L2.items():
        o[n + "2"] = np.ascontiguousarray(a)
    kv, kvb = L3.pop("kv_w"), L3.pop("kv_b")
    for j, n in enumerate("kv"):
        o[n + "_w3"] = np.ascontiguousarray(kv.reshape(E, E, 2)[..., j])
        o[n + "_b3"] = np.ascontiguousarray(kvb.reshape(E, 2)[..., j])
    for n, a in L3.items():
        o[n + "3"] = np.ascontiguousarray(a)
    o["mask1"] = np.ascontiguousarray(g["mask_BxS2_bf1"]).view(np.uint8)
    o["mask3"] = np.ascontiguousarray(g["mask_BxS2_ik0"])
    am = g["mask_Bx1xSxS2_ff0"][:, 0]
    o["mask2"] = np.ascontiguousarray(am)
    o["mask2_t"] = tr(am)
    i = np.arange(P)
    head, pos = i // HS, i % HS
    same = (head[:, None] == head[None, :])
    for n in ("ln1_w", "ln1_b", "ln2_w", "ln2_b", "maa_x", "time_decay", "gn_w", "gn_b", "ffn_maa_k", "ffn_maa_r", "faaaa",
              "ln_gamma1", "ln_beta1", "bq2", "bk2", "bo2", "gamma2", "beta2", "q_b3", "k_b3", "out_b3", "postnorm_w3",
              "mlp_b13", "mlp_b23"):
        o[n] = col(o[n])
    o["maa_stack"] = np.ascontiguousarray(o["maa_stack"].reshape(5, C, P).transpose(2, 0, 1))
    o["c_ident"] = np.eye(P, dtype=np.float32)
    o["c_head"] = same.astype(np.float32)
    d = np.arange(HS)
    o["c_sel"] = (same[:, None, :] & (pos[:, None, None] == d[None, :, None])).astype(np.float32)
    o["c_red"] = (same[:, None, :] & (pos[None, None, :] == d[None, :, None])).astype(np.float32)
    o["c_q"] = np.full((QUAD * T,), MASKED, np.float16)
    o["c_k"] = np.full((QUAD * (S2 + T),), -1.0, np.float16)
    o["c_ones"] = np.ones((P, 16, HS), np.float32)
    return o
```
